# Optimizing a Trainium2 kernel written in Bass

```python
import numpy as np
import jax
import jax.numpy as jnp

def _softmax(x, axis=-1):
    return jax.nn.softmax(x, axis=axis)

def _gelu(x):
    return jax.nn.gelu(x, approximate=True)

def _silu(x):
    return jax.nn.silu(x)

def _sigmoid(x):
    return jax.nn.sigmoid(x)

def _layernorm(x, axis=-1, eps=1e-05):
    m = jnp.mean(x, axis=axis, keepdims=True)
    v = jnp.var(x, axis=axis, keepdims=True)
    return (x - m) / jnp.sqrt(v + eps)

def _scatter_add(tgt, idx, src, axis=0):
    return tgt.at[idx].add(src)

def _segment_sum(src, seg, n):
    return jax.ops.segment_sum(src, seg, n)
kernel_name = 'mk_macaron_d1_jaxref_r2_28ac6e'

def setup_inputs(seed: int=0):
    np.random.seed(seed)
    _w = jnp.asarray

    def _L0_attn_setup():
        import jax, jax.numpy as jnp
        import numpy as np
        D_MODEL = 512
        D_STATE = 64
        EXPAND = 2
        D_INNER = D_MODEL * EXPAND
        DT_RANK = 32
        B, L = (4, 2048)
        key = jax.random.key(seed)
        ks = jax.random.split(key, 8)
        s = lambda fan_in: 1.0 / np.sqrt(fan_in)
        return {'x': jax.random.normal(ks[0], (B, L, D_MODEL), dtype=jnp.float32), 'W_in': jax.random.uniform(ks[1], (2 * D_INNER, D_MODEL), minval=-s(D_MODEL), maxval=s(D_MODEL)), 'conv_w': jax.random.uniform(ks[2], (D_INNER, 1, 4), minval=-s(4), maxval=s(4)), 'conv_b': jax.random.uniform(ks[3], (D_INNER,), minval=-s(4), maxval=s(4)), 'W_x': jax.random.uniform(ks[4], (DT_RANK + 2 * D_STATE, D_INNER), minval=-s(D_INNER), maxval=s(D_INNER)), 'W_dt': jax.random.uniform(ks[5], (D_INNER, DT_RANK), minval=-s(DT_RANK), maxval=s(DT_RANK)), 'b_dt': jax.random.uniform(ks[6], (D_INNER,), minval=-s(DT_RANK), maxval=s(DT_RANK)), 'W_out': jax.random.uniform(ks[7], (D_MODEL, D_INNER), minval=-s(D_INNER), maxval=s(D_INNER))}
    _L0_attn_in = _L0_attn_setup()

    def _L0_ffn_setup():
        import jax, jax.numpy as jnp
        import numpy as np
        NUM_EXPERTS = 64
        TOP_K = 8
        HIDDEN = 512
        INTER = 384
        BATCH, SEQ = (1, 512)
        CAPACITY = 128

        def _moe_forward(hidden_states, gate_w, w_gate, w_up, w_down):
            B, S, H = hidden_states.shape
            x = hidden_states.reshape(-1, H)
            T = x.shape[0]
            logits = (x @ gate_w.T).astype(jnp.float32)
            probs = jax.nn.softmax(logits, axis=-1)
            topk_p, topk_i = jax.lax.top_k(probs, TOP_K)
            topk_p = topk_p / jnp.sum(topk_p, axis=-1, keepdims=True)
            flat_e = topk_i.reshape(-1)
            onehot = jax.nn.one_hot(flat_e, NUM_EXPERTS, dtype=jnp.int32)
            pos_all = jnp.cumsum(onehot, axis=0) - 1
            pos = jnp.take_along_axis(pos_all, flat_e[:, None], axis=1)[:, 0]
            x_rep = jnp.repeat(x, TOP_K, axis=0)
            dispatch = jnp.zeros((NUM_EXPERTS, CAPACITY, H), x.dtype)
            dispatch = dispatch.at[flat_e, pos].set(x_rep, mode='drop')
            g = jax.nn.silu(jnp.einsum('ech,eih->eci', dispatch, w_gate))
            u = jnp.einsum('ech,eih->eci', dispatch, w_up)
            y = jnp.einsum('eci,ehi->ech', g * u, w_down)
            valid = pos < CAPACITY
            y_tok = y[flat_e, jnp.minimum(pos, CAPACITY - 1)]
            w = (topk_p.reshape(-1) * valid.astype(topk_p.dtype)).astype(x.dtype)
            out = (y_tok * w[:, None]).reshape(T, TOP_K, H).sum(axis=1)
            return out.reshape(B, S, H)
        key = jax.random.key(seed)
        k1, k2, k3, k4, k5 = jax.random.split(key, 5)
        scale = 0.02
        return {'hidden_states': jax.random.normal(k1, (BATCH, SEQ, HIDDEN), dtype=jnp.float32), 'gate_w': jax.random.normal(k2, (NUM_EXPERTS, HIDDEN), dtype=jnp.float32) * scale, 'w_gate': jax.random.normal(k3, (NUM_EXPERTS, INTER, HIDDEN), dtype=jnp.float32) * scale, 'w_up': jax.random.normal(k4, (NUM_EXPERTS, INTER, HIDDEN), dtype=jnp.float32) * scale, 'w_down': jax.random.normal(k5, (NUM_EXPERTS, HIDDEN, INTER), dtype=jnp.float32) * scale}
    _L0_ffn_in = _L0_ffn_setup()
    _d = {'L0_attn_x': _L0_attn_in['x'], 'L0_attn_W_in': _L0_attn_in['W_in'], 'L0_attn_conv_w': _L0_attn_in['conv_w'], 'L0_attn_conv_b': _L0_attn_in['conv_b'], 'L0_attn_W_x': _L0_attn_in['W_x'], 'L0_attn_W_dt': _L0_attn_in['W_dt'], 'L0_attn_b_dt': _L0_attn_in['b_dt'], 'L0_attn_W_out': _L0_attn_in['W_out'], 'L0_ffn_gate_w': _L0_ffn_in['gate_w'], 'L0_ffn_w_gate': _L0_ffn_in['w_gate'], 'L0_ffn_w_up': _L0_ffn_in['w_up'], 'L0_ffn_w_down': _L0_ffn_in['w_down']}
    _x0 = _d['L0_attn_x']
    _d['L0_attn_x'] = jax.random.normal(jax.random.fold_in(jax.random.key(seed), 1), (2, 4096, 512), dtype=_x0.dtype)
    del _x0
    return _d

def reference(L0_attn_x, L0_attn_W_in, L0_attn_conv_w, L0_attn_conv_b, L0_attn_W_x, L0_attn_W_dt, L0_attn_b_dt, L0_attn_W_out, L0_ffn_gate_w, L0_ffn_w_gate, L0_ffn_w_up, L0_ffn_w_down):

    def _L0_attn_ref(x, W_in, conv_w, conv_b, W_x, W_dt, b_dt, W_out):
        import jax, jax.numpy as jnp
        import numpy as np
        D_MODEL = 512
        D_STATE = 64
        EXPAND = 2
        D_INNER = D_MODEL * EXPAND
        DT_RANK = 32
        B, L = (4, 2048)
        Bsz, Lseq, _ = x.shape
        d_inner = W_in.shape[0] // 2
        shortcut = x
        xz = jnp.einsum('bld,ed->ble', x, W_in)
        xs, z = (xz[..., :d_inner], xz[..., d_inner:])
        xc = jax.lax.conv_general_dilated(xs.transpose(0, 2, 1), conv_w, (1,), [(3, 0)], dimension_numbers=('NCH', 'OIH', 'NCH'), feature_group_count=d_inner)
        xc = jax.nn.silu(xc + conv_b[None, :, None]).transpose(0, 2, 1)
        xp = jnp.einsum('ble,fe->blf', xc, W_x)
        dt = xp[..., :DT_RANK]
        a = jax.nn.softplus(jnp.einsum('blr,er->ble', dt, W_dt) + b_dt)
        y = xc * a
        out = jnp.einsum('ble,de->bld', y * jax.nn.silu(z), W_out)
        return out + shortcut

    def _L0_ffn_ref(hidden_states, gate_w, w_gate, w_up, w_down):
        import jax, jax.numpy as jnp
        import numpy as np
        NUM_EXPERTS = 64
        TOP_K = 8
        HIDDEN = 512
        INTER = 384
        BATCH, SEQ = (1, 512)
        CAPACITY = 128

        def _moe_forward(hidden_states, gate_w, w_gate, w_up, w_down):
            B, S, H = hidden_states.shape
            x = hidden_states.reshape(-1, H)
            T = x.shape[0]
            logits = (x @ gate_w.T).astype(jnp.float32)
            probs = jax.nn.softmax(logits, axis=-1)
            topk_p, topk_i = jax.lax.top_k(probs, TOP_K)
            topk_p = topk_p / jnp.sum(topk_p, axis=-1, keepdims=True)
            flat_e = topk_i.reshape(-1)
            onehot = jax.nn.one_hot(flat_e, NUM_EXPERTS, dtype=jnp.int32)
            pos_all = jnp.cumsum(onehot, axis=0) - 1
            pos = jnp.take_along_axis(pos_all, flat_e[:, None], axis=1)[:, 0]
            x_rep = jnp.repeat(x, TOP_K, axis=0)
            dispatch = jnp.zeros((NUM_EXPERTS, CAPACITY, H), x.dtype)
            dispatch = dispatch.at[flat_e, pos].set(x_rep, mode='drop')
            g = jax.nn.silu(jnp.einsum('ech,eih->eci', dispatch, w_gate))
            u = jnp.einsum('ech,eih->eci', dispatch, w_up)
            y = jnp.einsum('eci,ehi->ech', g * u, w_down)
            valid = pos < CAPACITY
            y_tok = y[flat_e, jnp.minimum(pos, CAPACITY - 1)]
            w = (topk_p.reshape(-1) * valid.astype(topk_p.dtype)).astype(x.dtype)
            out = (y_tok * w[:, None]).reshape(T, TOP_K, H).sum(axis=1)
            return out.reshape(B, S, H)
        return _moe_forward(hidden_states, gate_w, w_gate, w_up, w_down)
    x = L0_attn_x
    x = x + 0.5 * _L0_ffn_ref(_layernorm(x, axis=-1), L0_ffn_gate_w, L0_ffn_w_gate, L0_ffn_w_up, L0_ffn_w_down)
    x = x + _L0_attn_ref(_layernorm(x, axis=-1), L0_attn_W_in, L0_attn_conv_w, L0_attn_conv_b, L0_attn_W_x, L0_attn_W_dt, L0_attn_b_dt, L0_attn_W_out)
    x = x + 0.5 * _L0_ffn_ref(_layernorm(x, axis=-1), L0_ffn_gate_w, L0_ffn_w_gate, L0_ffn_w_up, L0_ffn_w_down)
    return x

_drawn_inputs = setup_inputs


def setup_inputs(seed=0):
    import zlib

    import numpy as np

    out = dict(_drawn_inputs(seed))
    spreads = {}
    factors = {'L0_attn_W_in': 3.644,
     'L0_attn_conv_w': 4.483,
     'L0_attn_conv_b': 5.594,
     'L0_attn_W_x': 8.0,
     'L0_attn_W_dt': 8.0,
     'L0_attn_b_dt': 48.508,
     'L0_attn_W_out': 3.426,
     'L0_ffn_gate_w': 8.0,
     'L0_ffn_w_gate': 8.0,
     'L0_ffn_w_up': 8.0,
     'L0_ffn_w_down': 8.0}
    for name, (base, spread) in spreads.items():
        noise = np.random.default_rng([zlib.crc32(name.encode()), seed]).standard_normal(out[name].shape)
        drawn = base * np.exp(spread * noise) if base else spread * noise
        out[name] = jnp.asarray(drawn.astype(out[name].dtype))
    for name, factor in factors.items():
        out[name] = (out[name] * factor).astype(out[name].dtype)
    return out
```

```python
from contextlib import ExitStack

import concourse.bass as bass
from concourse import mybir

F32 = mybir.dt.float32
F32R = mybir.dt.float32r
BF16 = mybir.dt.bfloat16
I32 = mybir.dt.int32
U8 = mybir.dt.uint8
ALU = mybir.AluOpType
ACT = mybir.ActivationFunctionType
AX = mybir.AxisListType

P = 128
GT = 4
GW = GT * P
TOP_K = 8
CAP = 128
EPS = 1e-5
NEG = -3.0e38
SOFTPLUS_CAP = 40.0


def wait(eng, sem, value):
    if not isinstance(value, int) or value > 0:
        eng.wait_ge(sem, value)


def run_passes(eng, n, body):
    body(0)
    if n > 2:
        with eng.Fori(1, n - 1) as i:
            body(i)
    if n > 1:
        body(n - 1)


def known(step):
    return isinstance(step, int)


def row_stats(dve, src, stats, mv):
    for j in range(GT):
        dve.bn_stats(stats[:, j, :], src[:, j, :])
    dve.drain()
    for j in range(GT):
        dve.bn_aggr(mv[:, j, 0:2], stats[:, j, :])
    dve.drain()
    return dve.tensor_scalar(mv[:, :, 2], mv[:, :, 1], EPS, None, ALU.add)


def rstd_of(pool, mv, minus_half, rstd):
    return pool.tensor_tensor(rstd[:, :], mv[:, :, 2], minus_half[:, :], ALU.pow)


def normalise(dve, src, xn, mv, rstd):
    for j in range(GT):
        last = dve.tensor_scalar(xn[:, j, :], src[:, j, :], mv[:, j, 0:1], rstd[:, j:j + 1],
                                 ALU.subtract, ALU.mult)
    return last


class Router:

    def __init__(self, sb, tag, E):
        self.logits = sb(tag + "logits", [P, GT, E], F32)
        self.top8 = sb(tag + "top8", [P, GT, TOP_K], F32)
        self.rest = sb(tag + "rest", [P, GT, E], F32)
        self.shifted = sb(tag + "shifted", [P, GT, E], F32)
        self.expd = sb(tag + "expd", [P, GT, E], F32)
        self.mask = sb(tag + "mask", [P, GT, E], F32)
        self.chosen = sb(tag + "chosen", [P, GT, E], BF16)
        self.total = sb(tag + "total", [P, GT], F32)
        self.table = sb(tag + "table", [P, GT, E + 2], F32)

    @staticmethod
    def flat(t):
        return t[:, :, :].rearrange("p j e -> p (j e)")

    def pick(self, dve, E):
        for j in range(GT):
            dve.max(self.top8[:, j, :], self.logits[:, j, :])
        dve.drain()
        for j in range(GT):
            dve.match_replace(self.rest[:, j, :], self.top8[:, j, :], self.logits[:, j, :], NEG)
        dve.tensor_tensor(self.shifted[:, :, :], self.logits[:, :, :],
                          self.top8[:, :, 0:1].broadcast_to([P, GT, E]), ALU.subtract)
        dve.drain()
        dve.tensor_tensor(self.mask[:, :, :], self.logits[:, :, :], self.rest[:, :, :], ALU.not_equal)
        return dve.tensor_tensor(self.chosen[:, :, :], self.logits[:, :, :], self.rest[:, :, :],
                                 ALU.not_equal)

    def tabulate(self, dve, E, mv, rstd):
        dve.tensor_tensor(self.expd[:, :, :], self.expd[:, :, :], self.mask[:, :, :], ALU.mult)
        dve.drain()
        dve.tensor_reduce(self.total[:, :], self.expd[:, :, :], AX.X, ALU.add)
        dve.drain()
        dve.reciprocal(self.total[:, :], self.total[:, :])
        dve.drain()
        dve.tensor_copy(self.table[:, :, E], mv[:, :, 0])
        dve.tensor_copy(self.table[:, :, E + 1], rstd[:, :])
        return dve.scalar_tensor_tensor(
            out=self.table[:, :, 0:E], in0=self.expd[:, :, :], scalar=0.5,
            in1=self.total[:, :].rearrange("p (j a) -> p j a", a=1).broadcast_to([P, GT, E]),
            op0=ALU.mult, op1=ALU.mult)


def build_program(nc, x, moe_w, gate_t, w_in, w_out, w_x, w_dt, conv_w, conv_b, b_dt, out):
    B, L, D = x.shape
    T = B * L
    E = gate_t.shape[2]
    KD = D // P
    MC = w_out.shape[1]
    DI = MC * P
    R = w_dt.shape[0]
    IN = (moe_w.shape[2] // (2 * KD + D // P)) if D == 512 else 0
    KI = IN // P
    NG = L // GW
    STEPS = B * NG
    TAPS = conv_w.shape[2]
    PAST = TAPS - 1
    assert B == 2 and E == 64 and 4 * R == P and GT * E <= 512 and D == 512
    assert moe_w.shape[2] == 2 * KD * IN + KI * D

    x_rows = x.rearrange("b l d -> (b l) d")
    out_rows = out.rearrange("b l d -> (b l) d")
    x1 = nc.dram_tensor("x1", [T, D], F32, kind="Internal").ap()
    x2 = nc.dram_tensor("x2", [T, D], F32, kind="Internal").ap()
    tab1 = nc.dram_tensor("tab1", [T, E + 2], F32, kind="Internal").ap()
    tab2 = nc.dram_tensor("tab2", [T, E + 2], F32, kind="Internal").ap()

    def group(rows, b, i):
        g = rows.rearrange("(b g j p) n -> b g p j n", b=B, j=GT, p=P)
        if known(i):
            return g[b, i]
        return g[b, bass.ds(i, 1)].rearrange("g p j n -> p (g j) n")

    with ExitStack() as top:
        def top_sb(name, shape, dt):
            return top.enter_context(nc.sbuf_tensor(name, shape, dt))

        ident = top_sb("ident", [P, P], F32)
        minus_half = top_sb("minus_half", [P, GT], F32)
        ident_b = top_sb("ident_b", [P, P], BF16)
        gate_sb = top_sb("gate_sb", [P, KD, E], F32)
        chosen_by = top_sb("chosen_by", [P, L], U8)
        slot_token = top_sb("slot_token", [P, E], I32)

        constants(nc, ident, ident_b, minus_half, gate_sb, gate_t)
        first_routing(nc, top, x_rows, x1, tab1, group, NG, KD, E, D, ident, ident_b, minus_half, gate_sb, chosen_by)
        find_slots(nc, T, L, E, ident, chosen_by, slot_token, "a")
        experts(nc, x_rows, tab1, x1, moe_w, T, E, D, KD, IN, KI, ident, slot_token, "a")
        mixer(nc, x1, x2, out_rows, tab2, group, NG, KD, MC, R, PAST, E, D, L, w_in, w_out, w_x, w_dt,
              conv_w, conv_b, b_dt, ident, ident_b, minus_half, gate_sb, chosen_by)
        find_slots(nc, T, L, E, ident, chosen_by, slot_token, "b")
        experts(nc, x2, tab2, out_rows, moe_w, T, E, D, KD, IN, KI, ident, slot_token, "b")


def constants(nc, ident, ident_b, minus_half, gate_sb, gate_t):
    with ExitStack() as ctx:
        made = ctx.enter_context(nc.semaphore("ident_made"))
        loaded = ctx.enter_context(nc.semaphore("gate_loaded"))
        block = ctx.enter_context(nc.Block())

        @block.gpsimd
        def _(pool):
            pool.memset(ident[:, :], 0.0).then_inc(made, 1)
            pool.memset(ident_b[:, :], 0.0).then_inc(made, 1)
            pool.wait_ge(made, 2)
            for m in (ident, ident_b):
                pool.affine_select(out=m[:, :], in_=m[:, :], compare_op=ALU.not_equal, fill=1.0,
                                   base=0, pattern=[[-1, P]], channel_multiplier=1).then_inc(made, 1)
            pool.memset(minus_half[:, :], -0.5).then_inc(made, 1)
            pool.wait_ge(made, 5)

        @block.sync
        def _(sp):
            sp.dma_start(gate_sb[:, :, :], gate_t).then_inc(loaded, 16)
            sp.wait_ge(loaded, 16)


def first_routing(nc, top, x_rows, x1, tab1, group, NG, KD, E, D, ident, ident_b, minus_half, gate_sb, chosen_by):
    with ExitStack() as ctx:
        def sb(name, shape, dt):
            return ctx.enter_context(nc.sbuf_tensor("r_" + name, shape, dt))

        def psum(name):
            return ctx.enter_context(nc.psum_tensor("r_" + name, [P, 512], F32))

        def sem(name):
            return ctx.enter_context(nc.semaphore("r_" + name))

        X = [sb(f"x{b}", [P, GT, D], F32) for b in range(2)]
        XN = [sb(f"xn{b}", [P, GT, D], F32) for b in range(2)]
        XT = [sb(f"xt{b}", [P, KD, GW], F32) for b in range(2)]
        stats = sb("stats", [P, GT, 6], F32)
        mv = [sb(f"mv{b}", [P, GT, 3], F32) for b in range(2)]
        rstd = [sb(f"rstd{b}", [P, GT], F32) for b in range(2)]
        rt = [Router(sb, f"rt{b}_", E) for b in range(2)]
        turn_ps = [psum(f"turn{n}") for n in range(2)]
        logit_ps = [psum(f"logit{b}") for b in range(2)]
        chosen_ps = [psum(f"chosen{b}") for b in range(2)]

        x_in = [sem(f"x_in{b}") for b in range(2)]
        var_made = sem("var_made")
        rstd_made = sem("rstd_made")
        xn_made = sem("xn_made")
        turned = sem("turned")
        xt_made = sem("xt_made")
        logits_done = sem("logits_done")
        chosen_made = sem("chosen_made")
        exp_made = sem("exp_made")
        chosen_turned = sem("chosen_turned")
        table_made = sem("table_made")
        table_out = [sem(f"table_out{b}") for b in range(2)]
        x1_filled = sem("x1_filled")
        block = ctx.enter_context(nc.Block())

        @block.sync
        def _(sp):
            for b in range(2):
                sp.dma_start(X[b][:, :, :], group(x_rows, b, 0)).then_inc(x_in[b], 16)
            sp.dma_start(x1.rearrange("(p r) d -> p (r d)", p=P),
                         x_rows.rearrange("(p r) d -> p (r d)", p=P)).then_inc(x1_filled, 16)

            def load_next(i):
                for b in range(2):
                    sp.wait_ge(xn_made, i * 2 + b + 1)
                    sp.dma_start(X[b][:, :, :], group(x_rows, b, i + 1)).then_inc(x_in[b], 16)
            run_passes(sp, NG - 1, load_next)
            sp.wait_ge(x1_filled, 16)

        @block.vector
        def _(dve):
            def one_pass(i):
                for b in range(2):
                    dve.wait_ge(x_in[b], i * 16 + 16)
                    row_stats(dve, X[b], stats, mv[b]).then_inc(var_made, 1)
                    dve.drain()
                for b in range(2):
                    dve.wait_ge(rstd_made, i * 2 + b + 1)
                    normalise(dve, X[b], XN[b], mv[b], rstd[b]).then_inc(xn_made, 1)
                for b in range(2):
                    s = i * 2 + b
                    r = rt[b]
                    dve.wait_ge(logits_done, s + 1)
                    dve.tensor_copy(r.flat(r.logits), logit_ps[b][:, 0:GT * E])
                    dve.drain()
                    r.pick(dve, E).then_inc(chosen_made, 1)
                    dve.wait_ge(exp_made, s + 1)
                    wait(dve, table_out[b], i * 16)
                    r.tabulate(dve, E, mv[b], rstd[b]).then_inc(table_made, 1)
                    dve.wait_ge(chosen_turned, s + 1)
                    h = slice(64 * b, 64 * b + 64)
                    dve.tensor_copy(chosen_by[h, bass.ds(i * GW, GW)], chosen_ps[b][h, :])
            run_passes(dve, NG, one_pass)

        @block.scalar
        def _(act):
            def one_pass(i):
                for b in range(2):
                    s = i * 2 + b
                    for k in range(KD):
                        act.wait_ge(turned, s * KD + k + 1)
                        act.activation(XT[b][:, k, :], turn_ps[k % 2][:, :], ACT.Copy)\
                           .then_inc(xt_made, 1)
                for b in range(2):
                    act.wait_ge(chosen_made, i * 2 + b + 1)
                    act.activation(rt[b].flat(rt[b].expd), rt[b].flat(rt[b].shifted), ACT.Exp)\
                       .then_inc(exp_made, 1)
            run_passes(act, NG, one_pass)

        @block.tensor
        def _(pe):
            def one_pass(i):
                for b in range(2):
                    s = i * 2 + b
                    pe.wait_ge(xn_made, s + 1)
                    for k in range(KD):
                        if b == 1 or k >= 2:
                            pe.wait_ge(xt_made, s * KD + k - 1)
                        for j in range(GT):
                            mm = pe.transpose(turn_ps[k % 2][:, j * P:(j + 1) * P],
                                              XN[b][:, j, k * P:(k + 1) * P], ident[:, :])
                        mm.then_inc(turned, 1)
                for b in range(2):
                    s = i * 2 + b
                    pe.wait_ge(xt_made, (s + 1) * KD)
                    logits(pe, logit_ps[b], XT[b], gate_sb, KD, E).then_inc(logits_done, 1)
                for b in range(2):
                    pe.wait_ge(chosen_made, i * 2 + b + 1)
                    turn_mask(pe, chosen_ps[b], rt[b], ident_b, b).then_inc(chosen_turned, 1)
            run_passes(pe, NG, one_pass)

        @block.gpsimd
        def _(pool):
            def one_pass(i):
                for b in range(2):
                    pool.wait_ge(var_made, i * 2 + b + 1)
                    rstd_of(pool, mv[b], minus_half, rstd[b]).then_inc(rstd_made, 1)
                for b in range(2):
                    pool.wait_ge(table_made, i * 2 + b + 1)
                    pool.dma_start(group(tab1, b, i), rt[b].table[:, :, :]).then_inc(table_out[b], 16)
            run_passes(pool, NG, one_pass)
            for b in range(2):
                pool.wait_ge(table_out[b], 16 * NG)


def logits(pe, bank, xt, gate_sb, KD, E):
    for j in range(GT):
        for k in range(KD):
            mm = pe.matmul(bank[:, j * E:(j + 1) * E], xt[:, k, j * P:(j + 1) * P], gate_sb[:, k, :],
                           start=(k == 0), stop=(k == KD - 1))
    return mm


def turn_mask(pe, bank, router, ident_b, b):
    for j in range(GT):
        mm = pe.matmul(bank[64 * b:64 * b + 64, j * P:(j + 1) * P], router.chosen[:, j, :],
                       ident_b[:, :], start=True, stop=True)
    return mm


def find_slots(nc, T, L, E, ident, chosen_by, slot_token, tag):
    with ExitStack() as ctx:
        def sb(name, shape, dt):
            return ctx.enter_context(nc.sbuf_tensor(f"f{tag}_{name}", shape, dt))

        def sem(name):
            return ctx.enter_context(nc.semaphore(f"f{tag}_{name}"))

        number = sb("number", [P, L], I32)
        keys = sb("keys", [P, L], F32)
        best = sb("best", [P, CAP], F32)
        both = sb("both", [E, 2 * CAP], F32)
        final = sb("final", [E, CAP], F32)
        raised = sb("raised", [P, E], F32)
        turned_ps = ctx.enter_context(nc.psum_tensor(f"f{tag}_turned", [P, E], F32))
        numbered = sem("numbered")
        final_made = sem("final_made")
        final_turned = sem("final_turned")
        block = ctx.enter_context(nc.Block())

        @block.gpsimd
        def _(pool):
            for b in range(2):
                pool.iota(number[64 * b:64 * b + 64, :], [[-1, L]], base=T - b * L,
                          channel_multiplier=0).then_inc(numbered, 1)

        @block.vector
        def _(dve):
            def take(keys, best, n):
                for r in range(n // TOP_K):
                    eight = best[:, r * TOP_K:(r + 1) * TOP_K]
                    dve.max(eight, keys)
                    dve.drain()
                    dve.match_replace(keys, eight, keys, 0.0)
                    dve.drain()

            dve.wait_ge(numbered, 2)
            dve.scalar_tensor_tensor(out=keys[:, :], in0=chosen_by[:, :], scalar=float(T),
                                     in1=number[:, :], op0=ALU.mult, op1=ALU.add)
            dve.drain()
            take(keys[:, :], best[:, :], CAP)
            for b in range(2):
                dve.tensor_copy(both[:, b * CAP:(b + 1) * CAP], best[64 * b:64 * b + 64, :])
            dve.drain()
            take(both[:, :], final[:, :], CAP)
            dve.drain().then_inc(final_made, 1)
            dve.wait_ge(final_turned, 1)
            dve.tensor_scalar(raised[:, :], turned_ps[:, :], float(T), float(T), ALU.is_gt, ALU.mult)
            dve.drain()
            dve.tensor_tensor(raised[:, :], raised[:, :], turned_ps[:, :], ALU.subtract)
            dve.drain()
            dve.tensor_scalar(slot_token[:, :], raised[:, :], float(T), None, ALU.add)

        @block.tensor
        def _(pe):
            pe.wait_ge(final_made, 1)
            pe.transpose(turned_ps[:, :], final[:, :], ident[0:E, 0:E]).then_inc(final_turned, 1)


def experts(nc, src, table, dst, moe_w, T, E, D, KD, IN, KI, ident, slot_token, tag):
    RING = 4
    EW = moe_w.shape[2]
    GU = KD * IN
    with ExitStack() as ctx:
        def sb(name, shape, dt):
            return ctx.enter_context(nc.sbuf_tensor(f"m{tag}_{name}", shape, dt))

        def psum(name, n):
            return ctx.enter_context(nc.psum_tensor(f"m{tag}_{name}", [P, n], F32))

        def sem(name):
            return ctx.enter_context(nc.semaphore(f"m{tag}_{name}"))

        W = [sb(f"w{k}", [P, EW], F32) for k in range(RING)]
        XG = [sb(f"xg{k}", [P, D], F32) for k in range(RING)]
        tab = [sb(f"tab{k}", [P, E + 2], F32) for k in range(RING)]
        fetched = [sb(f"fetched{k}", [P, 1], I32) for k in range(RING)]
        stored = [sb(f"stored{k}", [P, 1], I32) for k in range(RING)]
        zero = sb("zero", [P, 1], F32)
        mark = sb("mark", [P, 2 * RING], F32)
        XN = [sb(f"xn{k}", [P, D], F32) for k in range(2)]
        XT = [sb(f"xt{k}", [P, KD, P], F32) for k in range(2)]
        act_g = [sb(f"act_g{k}", [P, IN], F32) for k in range(2)]
        gu = [sb(f"gu{k}", [P, IN], F32) for k in range(2)]
        guT = [sb(f"guT{k}", [P, KI, P], F32) for k in range(2)]
        result = [sb(f"result{k}", [P, D], F32) for k in range(2)]
        x_ps = psum("x", D)
        gate_ps = psum("gate", IN)
        up_ps = psum("up", IN)
        gu_ps = psum("gu", IN)
        down_ps = [psum(f"down{k}", D) for k in range(2)]

        gate_in = [sem(f"gate_in{k}") for k in range(RING)]
        up_in = [sem(f"up_in{k}") for k in range(RING)]
        down_in = [sem(f"down_in{k}") for k in range(RING)]
        zeroed = sem("zeroed")
        held = sem("held")
        indexed = sem("indexed")
        stored_made = sem("stored_made")
        rows_in = [sem(f"rows_in{k}") for k in range(RING)]
        tab_in = [sem(f"tab_in{k}") for k in range(RING)]
        added = sem("added")
        xn_made = sem("xn_made")
        x_turned = sem("x_turned")
        xt_made = sem("xt_made")
        gate_done = sem("gate_done")
        up_done = sem("up_done")
        act_made = sem("act_made")
        gu_made = sem("gu_made")
        gu_turned = sem("gu_turned")
        guT_made = sem("guT_made")
        down_done = sem("down_done")
        result_made = sem("result_made")
        block = ctx.enter_context(nc.Block())

        def each(eng, body):
            def one_pass(i):
                for k in range(RING):
                    body(i, k, i * RING + k)
            run_passes(eng, E // RING, one_pass)

        def beyond(e):
            return known(e) and e >= E

        @block.sync
        def _(sp):
            def part(e, at, n):
                rows = moe_w[e] if known(e) else moe_w[bass.ds(e, 1)].rearrange("a p n -> p (a n)")
                return rows[:, at:at + n]

            def body(i, k, e):
                for at, n, done, landed in ((0, GU, gate_done, gate_in), (GU, GU, up_done, up_in),
                                            (2 * GU, KI * D, down_done, down_in)):
                    wait(sp, done, e - RING + 1)
                    sp.dma_start(W[k][:, at:at + n], part(e, at, n)).then_inc(landed[k], 16)
            each(sp, body)

        @block.gpsimd
        def _(pool):
            def hold(e, k, which):
                wait(pool, held, 2 * (e - RING) + which + 1)
                at = slice(2 * k + which, 2 * k + which + 1)
                pool.tensor_tensor(mark[:, at], zero[:, :], zero[:, :], ALU.add).then_inc(held, 1)

            def fetch(e, k):
                wait(pool, xn_made, e - RING + 1)
                pool.tensor_copy(fetched[k][:, :], slot_token[:, bass.ds(e, 1)]).then_inc(indexed, 1)
                pool.wait_ge(indexed, e + 1)
                hold(e, k, 0)
                for rows, there, landed in ((XG[k], src, rows_in[k]), (tab[k], table, tab_in[k])):
                    pool.indirect_dma_start(
                        out=rows[:, :], out_offset=None, in_=there,
                        in_offset=bass.IndirectOffsetOnAxis(ap=fetched[k][:, :], axis=0))\
                        .then_inc(landed, 16)

            pool.memset(zero[:, :], 0.0).then_inc(zeroed, 1)
            pool.wait_ge(zeroed, 1)
            for e in range(RING - 1):
                fetch(e, e)

            def body(i, k, e):
                pool.tensor_copy(stored[k][:, :], slot_token[:, bass.ds(e, 1)]).then_inc(stored_made, 1)
                if not beyond(e + RING - 1):
                    fetch(e + RING - 1, (k + RING - 1) % RING)
                pool.wait_ge(stored_made, e + 1)
                wait(pool, added, e * 16)
                pool.wait_ge(result_made, e + 1)
                hold(e, k, 1)
                pool.indirect_dma_start(
                    out=dst, out_offset=bass.IndirectOffsetOnAxis(ap=stored[k][:, :], axis=0),
                    in_=result[k % 2][:, :], in_offset=None, compute_op=ALU.add).then_inc(added, 16)
            each(pool, body)
            pool.wait_ge(added, 16 * E)

        @block.vector
        def _(dve):
            def norm(i, e, k):
                dve.wait_ge(rows_in[k], i * 16 + 16)
                wait(dve, x_turned, e - 1)
                dve.wait_ge(tab_in[k], i * 16 + 16)
                dve.tensor_scalar(XN[k % 2][:, :], XG[k][:, :], tab[k][:, E:E + 1],
                                  tab[k][:, E + 1:E + 2], ALU.subtract, ALU.mult).then_inc(xn_made, 1)

            def mul(e, k):
                dve.wait_ge(act_made, e + 1)
                dve.wait_ge(up_done, e + 1)
                dve.tensor_tensor(gu[k % 2][:, :], act_g[k % 2][:, :], up_ps[:, :], ALU.mult)\
                   .then_inc(gu_made, 1)

            norm(0, 0, 0)
            norm(0, 1, 1)
            mul(0, 0)

            def body(i, k, e):
                if not beyond(e + 2):
                    norm(i + (k + 2) // RING, e + 2, (k + 2) % RING)
                if not beyond(e + 1):
                    mul(e + 1, k + 1)
                dve.wait_ge(down_done, e + 1)
                wait(dve, added, (e - 1) * 16)
                dve.tensor_scalar(result[k % 2][:, :], down_ps[k % 2][:, :],
                                  tab[k][:, bass.ds(e, 1)], None, ALU.mult).then_inc(result_made, 1)
            each(dve, body)

        @block.scalar
        def _(act):
            def copy_xt(e, k):
                act.wait_ge(x_turned, e + 1)
                act.activation(XT[k % 2][:, :, :].rearrange("p k c -> p (k c)"), x_ps[:, :], ACT.Copy)\
                   .then_inc(xt_made, 1)

            def silu(e, k):
                act.wait_ge(gate_done, e + 1)
                act.activation(act_g[k % 2][:, :], gate_ps[:, :], ACT.Silu).then_inc(act_made, 1)

            copy_xt(0, 0)
            silu(0, 0)
            copy_xt(1, 1)

            def body(i, k, e):
                if not beyond(e + 1):
                    silu(e + 1, k + 1)
                act.wait_ge(gu_turned, e + 1)
                act.activation(guT[k % 2][:, :, :].rearrange("p k c -> p (k c)"), gu_ps[:, :], ACT.Copy)\
                   .then_inc(guT_made, 1)
                if not beyond(e + 2):
                    copy_xt(e + 2, k)
            each(act, body)

        @block.tensor
        def _(pe):
            def turn_x(e, k):
                pe.wait_ge(xn_made, e + 1)
                for c in range(KD):
                    mm = pe.transpose(x_ps[:, c * P:(c + 1) * P], XN[k % 2][:, c * P:(c + 1) * P],
                                      ident[:, :])
                mm.then_inc(x_turned, 1)

            def project(bank, k, part):
                w = W[k % RING]
                for c in range(KD):
                    at = part * GU + c * IN
                    mm = pe.matmul(bank[:, :], XT[k % 2][:, c, :], w[:, at:at + IN],
                                   start=(c == 0), stop=(c == KD - 1))
                return mm

            def gate(i, e, k):
                pe.wait_ge(gate_in[k % RING], i * 16 + 16)
                pe.wait_ge(xt_made, e + 1)
                wait(pe, act_made, e)
                project(gate_ps, k, 0).then_inc(gate_done, 1)

            def up(i, e, k):
                pe.wait_ge(up_in[k % RING], i * 16 + 16)
                project(up_ps, k, 1).then_inc(up_done, 1)

            turn_x(0, 0)
            gate(0, 0, 0)
            up(0, 0, 0)
            turn_x(1, 1)

            def body(i, k, e):
                if not beyond(e + 1):
                    gate(i + (k + 1) // RING, e + 1, k + 1)
                pe.wait_ge(gu_made, e + 1)
                for c in range(KI):
                    mm = pe.transpose(gu_ps[:, c * P:(c + 1) * P], gu[k % 2][:, c * P:(c + 1) * P],
                                      ident[:, :])
                mm.then_inc(gu_turned, 1)
                if not beyond(e + 1):
                    up(i + (k + 1) // RING, e + 1, k + 1)
                if not beyond(e + 2):
                    turn_x(e + 2, k)
                pe.wait_ge(guT_made, e + 1)
                pe.wait_ge(down_in[k], i * 16 + 16)
                wait(pe, result_made, e - 1)
                for c in range(KI):
                    at = 2 * GU + c * D
                    mm = pe.matmul(down_ps[k % 2][:, :], guT[k % 2][:, c, :], W[k][:, at:at + D],
                                   start=(c == 0), stop=(c == KI - 1))
                mm.then_inc(down_done, 1)
            each(pe, body)


def mixer(nc, x1, x2, out_rows, tab2, group, NG, KD, MC, R, PAST, E, D, L, w_in, w_out, w_x, w_dt,
          conv_w, conv_b, b_dt, ident, ident_b, minus_half, gate_sb, chosen_by):
    STEPS = 2 * NG
    DI = MC * P
    XT_TURNS = (0, 2, 4, 5)
    assert len(XT_TURNS) == KD
    with ExitStack() as ctx:
        def sb(name, shape, dt):
            return ctx.enter_context(nc.sbuf_tensor("c_" + name, shape, dt))

        def psum(name):
            return ctx.enter_context(nc.psum_tensor("c_" + name, [P, GW], F32))

        def sem(name):
            return ctx.enter_context(nc.semaphore("c_" + name))

        w_in_hi = sb("w_in_hi", [P, KD, 2 * DI], F32R)
        w_in_lo = sb("w_in_lo", [P, KD, 2 * DI], F32R)
        w_out_hi = sb("w_out_hi", [P, MC, D], F32R)
        w_out_lo = sb("w_out_lo", [P, MC, D], F32R)
        w_x_hi = sb("w_x_hi", [P, MC, P], F32R)
        w_x_lo = sb("w_x_lo", [P, MC, P], F32R)
        w_dt_parts = sb("w_dt_parts", [P, DI], F32R)
        taps = sb("taps", [P, MC, PAST + 1], F32)
        conv_bias = sb("conv_bias", [P, MC], F32)
        dt_bias = sb("dt_bias", [P, MC], F32)
        X = [sb(f"x{b}", [P, GT, D], F32) for b in range(2)]
        XN = sb("xn", [P, GT, D], F32)
        xt_hi = sb("xt_hi", [P, KD, GW], F32R)
        xt_lo = sb("xt_lo", [P, KD, GW], F32R)
        x2t = sb("x2t", [P, KD, GW], F32)
        gated = sb("gated", [P, MC, GW], F32)
        half_hi = [sb(f"half_hi{k}", [P, GW], F32R) for k in range(2)]
        half_lo = [sb(f"half_lo{k}", [P, GW], F32R) for k in range(2)]
        xs = [sb(f"xs{k}", [P, PAST + GW], F32) for k in range(2)]
        temp = [sb(f"temp{k}", [P, GW], F32) for k in range(2)]
        silu_z = [sb(f"silu_z{k}", [P, GW], F32) for k in range(2)]
        chain = temp + silu_z
        dt_parts = sb("dt_parts", [P, GW], F32R)
        past = [sb(f"past{b}", [P, MC, PAST], F32) for b in range(2)]
        stats = sb("stats", [P, GT, 6], F32)
        mv, mv2 = (sb(f"mv{n}", [P, GT, 3], F32) for n in (1, 2))
        rstd, rstd2 = (sb(f"rstd{n}", [P, GT], F32) for n in (1, 2))
        router = Router(sb, "rt_", E)

        with ExitStack() as prep:
            landed = [prep.enter_context(nc.semaphore(f"p_landed{k}")) for k in range(2)]
            small_in = prep.enter_context(nc.semaphore("p_small_in"))
            hi_made = prep.enter_context(nc.semaphore("p_hi_made"))
            lo_made = prep.enter_context(nc.semaphore("p_lo_made"))
            block = prep.enter_context(nc.Block())
            stage = [X[k][:, :, :].rearrange("p j d -> p (j d)") for k in range(2)]
            flat = "p k n -> p (k n)"
            half = MC // 2
            assert 2 * DI == GT * D and half * D == GT * D and MC * P <= GT * D and DI <= GT * D
            pieces = [(w_in[:, k, :], w_in_hi[:, k, :], w_in_lo[:, k, :]) for k in range(KD)]
            pieces += [(w_out[:, h * half:(h + 1) * half, :].rearrange(flat),
                        w_out_hi[:, h * half:(h + 1) * half, :].rearrange(flat),
                        w_out_lo[:, h * half:(h + 1) * half, :].rearrange(flat)) for h in range(2)]
            N = len(pieces)

            @block.sync
            def _(sp):
                for n, (src, _, _) in enumerate(pieces):
                    wait(sp, lo_made, n - 1)
                    sp.dma_start(stage[n % 2], src).then_inc(landed[n % 2], 16)
                sp.wait_ge(lo_made, N)
                for c in range(4):
                    dst = stage[0][:, 0:MC * P].rearrange("p (m c r) -> p m c r", m=MC, c=4)
                    sp.dma_start(dst[:, :, c, :], w_x).then_inc(landed[0], 16)
                    sp.dma_start(stage[1][c * R:(c + 1) * R, 0:DI], w_dt).then_inc(landed[1], 16)
                for dst, src in ((taps, conv_w), (conv_bias, conv_b), (dt_bias, b_dt)):
                    sp.dma_start(dst[:], src).then_inc(small_in, 16)
                sp.wait_ge(small_in, 48)

            def last_landed(eng):
                eng.wait_ge(landed[0], 16 * (N // 2 + 4))
                eng.wait_ge(landed[1], 16 * (N // 2 + 4))

            @block.scalar
            def _(act):
                for n, (_, hi, _) in enumerate(pieces):
                    act.wait_ge(landed[n % 2], 16 * (n // 2 + 1))
                    act.activation(hi, stage[n % 2], ACT.Copy).then_inc(hi_made, 1)
                last_landed(act)
                act.activation(w_x_hi[:, :, :].rearrange(flat), stage[0][:, 0:MC * P], ACT.Copy)\
                   .then_inc(hi_made, 1)
                act.activation(w_dt_parts[:, :], stage[1][:, 0:DI], ACT.Copy).then_inc(hi_made, 1)

            @block.vector
            def _(dve):
                for b in range(2):
                    dve.memset(past[b][:, :, :], 0.0)
                for n, (_, hi, lo) in enumerate(pieces):
                    dve.wait_ge(hi_made, n + 1)
                    dve.tensor_tensor(lo, stage[n % 2], hi, ALU.subtract).then_inc(lo_made, 1)
                dve.wait_ge(hi_made, N + 2)
                dve.tensor_tensor(w_x_lo[:, :, :].rearrange(flat), stage[0][:, 0:MC * P],
                                  w_x_hi[:, :, :].rearrange(flat), ALU.subtract)
                low = slice(2 * R, 4 * R)
                dve.tensor_tensor(w_dt_parts[low, :], stage[1][low, 0:DI], w_dt_parts[low, :],
                                  ALU.subtract)

        chunk_ps = [psum(f"chunk{k}") for k in range(2)]
        dt_ps = psum("dt")
        v_ps = [dt_ps] + chunk_ps
        turn_ps = psum("turn")
        out_ps = [psum(f"out{j}") for j in range(GT)]

        x_in = [sem(f"x_in{b}") for b in range(2)]
        var_made = sem("var_made")
        rstd_made = sem("rstd_made")
        xn_made = sem("xn_made")
        res_made = sem("res_made")
        turned = sem("turned")
        xt_hi_made = sem("xt_hi_made")
        xt_made = sem("xt_made")
        xs_done = sem("xs_done")
        xs_read = sem("xs_read")
        past_in = sem("past_in")
        conv_made = sem("conv_made")
        xc_hi_made = sem("xc_hi_made")
        xc_made = sem("xc_made")
        xp_done = sem("xp_done")
        dt_hi_made = sem("dt_hi_made")
        dt_made = sem("dt_made")
        z_done = sem("z_done")
        z_read = sem("z_read")
        gate_made = sem("gate_made")
        v_done = sem("v_done")
        v_capped = sem("v_capped")
        exp_done = sem("exp_done")
        log_done = sem("log_done")
        v_read = sem("v_read")
        y_made = sem("y_made")
        y_hi_made = sem("y_hi_made")
        y_parts_made = sem("y_parts_made")
        out_done = sem("out_done")
        x2_made = sem("x2_made")
        x2_out = [sem(f"x2_out{b}") for b in range(2)]
        var2_made = sem("var2_made")
        rstd2_made = sem("rstd2_made")
        xn2_made = sem("xn2_made")
        turned2 = sem("turned2")
        x2t_made = sem("x2t_made")
        logits_done = sem("logits_done")
        logits_read = sem("logits_read")
        chosen_made = sem("chosen_made")
        chosen_turned = sem("chosen_turned")
        chosen_read = sem("chosen_read")
        exps_made = sem("exps_made")
        table_made = sem("table_made")
        table_out = sem("table_out")
        block = ctx.enter_context(nc.Block())

        def each(eng, body):
            def one_pass(i):
                for b in range(2):
                    body(i * 2 + b, i, b)
            run_passes(eng, NG, one_pass)
            body(STEPS, NG, 0)

        def first(s):
            return known(s) and s == 0

        def over(s):
            return known(s) and s >= STEPS

        def before(i, b):
            return (i, 0) if b == 1 else (i - 1, 1)

        @block.sync
        def _(sp):
            sp.dma_start(X[0][:, :, :], group(x1, 0, 0)).then_inc(x_in[0], 16)
            sp.dma_start(X[1][:, :, :], group(x1, 1, 0)).then_inc(x_in[1], 16)

            def body(s, i, b):
                if not first(s):
                    pi, pb = before(i, b)
                    if not over(s + 1):
                        sp.wait_ge(xn2_made, s)
                        sp.wait_ge(x2_out[pb], pi * 32 + 32)
                        sp.dma_start(X[pb][:, :, :], group(x1, pb, pi + 1)).then_inc(x_in[pb], 16)
            each(sp, body)
            for b in range(2):
                sp.wait_ge(x2_out[b], 32 * NG)
            sp.wait_ge(table_out, 16 * STEPS)

        def norm1(dve, s, i, b):
            dve.wait_ge(x_in[b], i * 16 + 16)
            row_stats(dve, X[b], stats, mv).then_inc(var_made, 1)
            dve.drain()
            dve.wait_ge(rstd_made, s + 1)
            normalise(dve, X[b], XN, mv, rstd).then_inc(xn_made, 1)

        def low_xt(dve, s, k):
            dve.wait_ge(xt_hi_made, s * KD + k + 1)
            dve.tensor_tensor(xt_lo[:, k, :], turn_ps[:, :], xt_hi[:, k, :], ALU.subtract)\
               .then_inc(xt_made, 1)

        @block.vector
        def _(dve):
            norm1(dve, 0, 0, 0)
            for k in range(KD):
                low_xt(dve, 0, k)

            def take_past(c, m, b):
                wait(dve, conv_made, c - 1)
                dve.tensor_copy(xs[m % 2][:, 0:PAST], past[b][:, m, :]).then_inc(past_in, 1)

            def convolve(c, m, b):
                t = temp[m % 2][:, :]
                dve.wait_ge(xs_read, c + 1)
                dve.wait_ge(past_in, c + 1)
                for tap in range(PAST):
                    conv = dve.scalar_tensor_tensor(
                        out=t, in0=xs[m % 2][:, tap:tap + GW], scalar=taps[:, m, tap:tap + 1],
                        in1=t, op0=ALU.mult, op1=ALU.add)
                    if tap < PAST - 1:
                        dve.drain()
                conv.then_inc(conv_made, 1)
                if m + 2 < MC:
                    take_past(c + 2, m + 2, b)

            def cap(v, m):
                dve.wait_ge(v_done, v + 1)
                if m >= 4:
                    dve.wait_ge(y_made, v - 3)
                dve.tensor_scalar(chain[m % 4][:, :], v_ps[m % 3][:, :], dt_bias[:, m:m + 1],
                                  SOFTPLUS_CAP, ALU.add, ALU.min).then_inc(v_capped, 1)

            def softplus(v, m):
                t = chain[m % 4][:, :]
                dve.wait_ge(log_done, v + 1)
                dve.scalar_tensor_tensor(out=t, in0=v_ps[m % 3][:, :], scalar=dt_bias[:, m:m + 1],
                                         in1=t, op0=ALU.add, op1=ALU.max).then_inc(v_read, 1)
                dve.wait_ge(v_read, v + 1)
                dve.wait_ge(gate_made, v + 1)
                dve.tensor_tensor(gated[:, m, :], gated[:, m, :], t, ALU.mult).then_inc(y_made, 1)

            for m in range(2):
                take_past(m, m, 0)

            def body(s, i, b):
                pi, pb = before(i, b)
                if not first(s):
                    dve.wait_ge(out_done, s * MC)
                    for j in range(GT):
                        last = dve.tensor_tensor(X[pb][:, j, :], X[pb][:, j, :], out_ps[j][:, :], ALU.add)
                    last.then_inc(x2_made, 1)
                    dve.drain()
                    row_stats(dve, X[pb], stats, mv2).then_inc(var2_made, 1)
                if not over(s):
                    convolve(s * MC, 0, b)
                if not first(s):
                    if over(s):
                        dve.drain()
                    else:
                        wait(dve, turned, s * KD + KD)
                    dve.wait_ge(rstd2_made, s)
                    normalise(dve, X[pb], XN, mv2, rstd2).then_inc(xn2_made, 1)
                if not over(s):
                    for m in range(1, MC):
                        convolve(s * MC + m, m, b)
                if not first(s):
                    dve.wait_ge(logits_done, s)
                    dve.tensor_copy(router.flat(router.logits), turn_ps[:, 0:GT * E])\
                       .then_inc(logits_read, 1)
                    dve.drain()
                    router.pick(dve, E).then_inc(chosen_made, 1)
                if not over(s):
                    dve.wait_ge(dt_hi_made, s + 1)
                    for c in (1, 3):
                        rows = slice(c * R, (c + 1) * R)
                        low = dve.tensor_tensor(dt_parts[rows, :], dt_ps[rows, :], dt_parts[rows, :],
                                                ALU.subtract)
                    low.then_inc(dt_made, 1)
                nb = 1 - b
                if not over(s + 1):
                    if first(s):
                        dve.wait_ge(turned, KD)
                        dve.wait_ge(res_made, 1)
                    norm1(dve, s + 1, i + b, nb)
                if not first(s):
                    dve.wait_ge(chosen_turned, s)
                    h = slice(64 * pb, 64 * pb + 64)
                    dve.tensor_copy(chosen_by[h, bass.ds(pi * GW, GW)], turn_ps[h, :])\
                       .then_inc(chosen_read, 1)
                if not over(s):
                    v = s * MC
                    cap(v, 0)
                    cap(v + 1, 1)
                    dve.wait_ge(gate_made, v + MC)
                    cap(v + 2, 2)
                    for m in range(MC):
                        softplus(v + m, m)
                        if 3 <= m + 2 < MC:
                            cap(v + m + 2, m + 2)
                        if not over(s + 1) and m - 1 in XT_TURNS:
                            low_xt(dve, s + 1, XT_TURNS.index(m - 1))
                if not first(s):
                    dve.wait_ge(exps_made, s)
                    wait(dve, table_out, (s - 1) * 16)
                    router.tabulate(dve, E, mv2, rstd2).then_inc(table_made, 1)
                if not over(s + 1):
                    for m in range(2):
                        take_past((s + 1) * MC + m, m, nb)
            each(dve, body)

        @block.scalar
        def _(act):
            def high_xt(s, k):
                act.wait_ge(turned, s * KD + k + 1)
                act.activation(xt_hi[:, k, :], turn_ps[:, :], ACT.Copy).then_inc(xt_hi_made, 1)

            def copy_x2t(s, k):
                act.wait_ge(turned2, (s - 1) * KD + k + 1)
                act.activation(x2t[:, k, :], turn_ps[:, :], ACT.Copy).then_inc(x2t_made, 1)

            def silu_xc(c, m):
                act.wait_ge(conv_made, c + 1)
                act.activation(gated[:, m, :], temp[m % 2][:, :], ACT.Silu)
                if m < 2:
                    wait(act, out_done, c - 1)
                else:
                    act.wait_ge(xp_done, c - 1)
                act.activation(half_hi[m % 2][:, :], temp[m % 2][:, :], ACT.Silu)\
                   .then_inc(xc_hi_made, 1)

            def high_y(v, m):
                act.wait_ge(y_made, v + 1)
                if m >= 2:
                    act.wait_ge(out_done, v - 1)
                act.activation(half_hi[m % 2][:, :], gated[:, m, :], ACT.Copy).then_inc(y_hi_made, 1)

            for k in range(KD):
                high_xt(0, k)

            def body(s, i, b):
                for m in range(MC):
                    c = s * MC + m
                    if not first(s) and m >= 5:
                        copy_x2t(s, m - 5)
                    if not over(s):
                        act.wait_ge(xs_done, c + 1)
                        wait(act, conv_made, c - 1)
                        act.activation(xs[m % 2][:, PAST:PAST + GW], chunk_ps[m % 2][:, :], ACT.Copy)
                        act.wait_ge(past_in, c + 1)
                        act.activation(past[b][:, m, :], chunk_ps[m % 2][:, GW - PAST:GW], ACT.Copy)
                        if m < 2:
                            wait(act, y_made, c - 1)
                        else:
                            act.wait_ge(xc_hi_made, c - 1)
                        act.activation(temp[m % 2][:, :], chunk_ps[m % 2][:, :], ACT.Identity,
                                       bias=conv_bias[:, m:m + 1], scale=taps[:, m, PAST:PAST + 1])\
                           .then_inc(xs_read, 1)
                        if m >= 1:
                            silu_xc(c - 1, m - 1)
                if not first(s):
                    copy_x2t(s, KD - 1)
                if not over(s):
                    silu_xc(s * MC + MC - 1, MC - 1)
                    for m in range(MC):
                        c = s * MC + m
                        act.wait_ge(z_done, c + 1)
                        wait(act, gate_made, c - 1)
                        act.activation(silu_z[m % 2][:, :], chunk_ps[m % 2][:, :], ACT.Silu)\
                           .then_inc(z_read, 1)
                        if m == 4:
                            act.wait_ge(xp_done, (s + 1) * MC)
                            act.activation(dt_parts[:, :], dt_ps[:, :], ACT.Copy)\
                               .then_inc(dt_hi_made, 1)
                def exps():
                    act.wait_ge(chosen_made, s)
                    act.activation(router.flat(router.expd), router.flat(router.shifted), ACT.Exp)\
                       .then_inc(exps_made, 1)

                if over(s):
                    exps()
                    return
                act.preload_act_table_set("natural_log_exp_and_others")
                for m in range(MC):
                    v = s * MC + m
                    if m >= 2:
                        high_y(v - 2, m - 2)
                        if not over(s + 1) and m - 2 in XT_TURNS:
                            high_xt(s + 1, XT_TURNS.index(m - 2))
                    act.wait_ge(v_capped, v + 1)
                    act.activation(chain[m % 4][:, :], chain[m % 4][:, :], ACT.Exp).then_inc(exp_done, 1)
                    act.wait_ge(exp_done, v + 1)
                    act.activation(chain[m % 4][:, :], chain[m % 4][:, :], ACT.Ln, bias=1.0)\
                       .then_inc(log_done, 1)
                    if m == 3 and not first(s):
                        exps()
                high_y(s * MC + MC - 2, MC - 2)
                high_y(s * MC + MC - 1, MC - 1)
            each(act, body)

        @block.gpsimd
        def _(pool):
            pool.wait_ge(var_made, 1)
            rstd_of(pool, mv, minus_half, rstd).then_inc(rstd_made, 1)
            pool.wait_ge(xn_made, 1)
            pool.tensor_tensor(X[0][:, :, :], X[0][:, :, :], XN[:, :, :], ALU.add).then_inc(res_made, 1)

            def store_table(s, pi, pb):
                pool.wait_ge(table_made, s)
                pool.dma_start(group(tab2, pb, pi), router.table[:, :, :]).then_inc(table_out, 16)

            def body(s, i, b):
                if not first(s):
                    pool.wait_ge(var2_made, s)
                    rstd_of(pool, mv2, minus_half, rstd2).then_inc(rstd2_made, 1)
                    pi, pb = before(i, b)
                    pool.dma_start(group(x2, pb, pi), X[pb][:, :, :]).then_inc(x2_out[pb], 16)
                    pool.dma_start(group(out_rows, pb, pi), X[pb][:, :, :]).then_inc(x2_out[pb], 16)
                if over(s):
                    store_table(s, pi, pb)
                    return
                for m in range(MC):
                    pool.wait_ge(xc_hi_made, s * MC + m + 1)
                    pool.tensor_tensor(half_lo[m % 2][:, :], gated[:, m, :], half_hi[m % 2][:, :],
                                       ALU.subtract).then_inc(xc_made, 1)
                for m in range(MC):
                    c = s * MC + m
                    pool.wait_ge(z_read, c + 1)
                    pool.wait_ge(xc_made, c + 1)
                    pool.tensor_tensor(gated[:, m, :], gated[:, m, :], silu_z[m % 2][:, :], ALU.mult)\
                        .then_inc(gate_made, 1)
                    if m == 4 and not over(s + 1):
                        pool.wait_ge(var_made, s + 2)
                        rstd_of(pool, mv, minus_half, rstd).then_inc(rstd_made, 1)
                for m in range(MC):
                    v = s * MC + m
                    pool.wait_ge(y_hi_made, v + 1)
                    pool.tensor_tensor(half_lo[m % 2][:, :], gated[:, m, :], half_hi[m % 2][:, :],
                                       ALU.subtract).then_inc(y_parts_made, 1)
                    if not over(s + 1) and m < GT:
                        if m == 0:
                            pool.wait_ge(xn_made, s + 2)
                        n = 1 - b
                        part = pool.tensor_tensor(X[n][:, m, :], X[n][:, m, :], XN[:, m, :], ALU.add)
                        if m == GT - 1:
                            part.then_inc(res_made, 1)
                if not first(s):
                    store_table(s, pi, pb)
            each(pool, body)

        @block.tensor
        def _(pe):
            def three(bank, a, b, start, stop):
                pe.matmul(bank, a[0], b[0], start=start, stop=False)
                pe.matmul(bank, a[0], b[1], start=False, stop=False)
                return pe.matmul(bank, a[1], b[0], start=False, stop=stop)

            def turn(src, k):
                for j in range(GT):
                    mm = pe.transpose(turn_ps[:, j * P:(j + 1) * P], src[:, j, k * P:(k + 1) * P],
                                      ident[:, :])
                return mm

            def turn_xt(s, k):
                if k == 0:
                    pe.wait_ge(xn_made, s + 1)
                    wait(pe, chosen_read, s - 1)
                else:
                    pe.wait_ge(xt_made, s * KD + k)
                turn(XN, k).then_inc(turned, 1)

            def in_proj(m):
                for k in range(KD):
                    cols = slice(m * P, (m + 1) * P)
                    mm = three(chunk_ps[m % 2][:, :], (w_in_hi[:, k, cols], w_in_lo[:, k, cols]),
                               (xt_hi[:, k, :], xt_lo[:, k, :]), k == 0, k == KD - 1)
                return mm

            def x_proj(s, m):
                wx, hi, lo = (w_x_hi[:, m, :], w_x_lo[:, m, :]), half_hi[m % 2], half_lo[m % 2]
                pe.wait_ge(xc_hi_made, s * MC + m + 1)
                pe.matmul(dt_ps[:, :], wx[0], hi[:, :], start=m == 0, stop=False)
                pe.matmul(dt_ps[:, :], wx[1], hi[:, :], start=False, stop=False)
                pe.wait_ge(xc_made, s * MC + m + 1)
                pe.matmul(dt_ps[:, :], wx[0], lo[:, :], start=False, stop=m == MC - 1)\
                    .then_inc(xp_done, 1)

            def out_proj(s, m):
                pe.wait_ge(y_hi_made, s * MC + m + 1)
                if m == 0:
                    wait(pe, x2_made, s)
                for j in range(GT):
                    hi = half_hi[m % 2][:, j * P:(j + 1) * P]
                    pe.matmul(out_ps[j][:, :], hi, w_out_hi[:, m, :], start=m == 0, stop=False)
                    pe.matmul(out_ps[j][:, :], hi, w_out_lo[:, m, :], start=False, stop=False)
                pe.wait_ge(y_parts_made, s * MC + m + 1)
                for j in range(GT):
                    mm = pe.matmul(out_ps[j][:, :], half_lo[m % 2][:, j * P:(j + 1) * P],
                                   w_out_hi[:, m, :], start=False, stop=m == MC - 1)
                mm.then_inc(out_done, 1)

            def dt_proj(s, m):
                v = s * MC + m
                if m == 0:
                    pe.wait_ge(dt_made, s + 1)
                elif m < 3:
                    pe.wait_ge(z_read, s * MC + MC - 2 + m)
                else:
                    pe.wait_ge(v_read, v - 2)
                pe.matmul(v_ps[m % 3][:, :], w_dt_parts[:, m * P:(m + 1) * P], dt_parts[:, :],
                          start=True, stop=True).then_inc(v_done, 1)

            for k in range(KD):
                turn_xt(0, k)

            def body(s, i, b):
                pb = before(i, b)[1]
                for m in range(MC):
                    if not over(s):
                        c = s * MC + m
                        if m == 0:
                            pe.wait_ge(xt_made, (s + 1) * KD)
                            wait(pe, v_read, s * MC)
                        elif m >= 2:
                            pe.wait_ge(xs_read, c - 1)
                        in_proj(m).then_inc(xs_done, 1)
                        if m >= 3:
                            x_proj(s, m - 3)
                    if not first(s) and m >= MC - KD:
                        k = m - (MC - KD)
                        if k == 0:
                            pe.wait_ge(xn2_made, s)
                            if over(s):
                                pe.wait_ge(xt_made, s * KD)
                        else:
                            pe.wait_ge(x2t_made, (s - 1) * KD + k)
                        turn(XN, k).then_inc(turned2, 1)
                for m in range(MC):
                    if not over(s):
                        c = s * MC + m
                        if m < 2:
                            pe.wait_ge(xs_read, c + MC - 1)
                        else:
                            pe.wait_ge(z_read, c - 1)
                        in_proj(MC + m).then_inc(z_done, 1)
                        if m < 3:
                            x_proj(s, MC - 3 + m)
                        if m == MC - 2:
                            dt_proj(s, 0)
                    if not first(s) and m == 0:
                        pe.wait_ge(x2t_made, s * KD)
                        logits(pe, turn_ps, x2t, gate_sb, KD, E).then_inc(logits_done, 1)
                    if not first(s) and m == 5:
                        pe.wait_ge(chosen_made, s)
                        turn_mask(pe, turn_ps, router, ident_b, pb).then_inc(chosen_turned, 1)
                if over(s):
                    return
                dt_proj(s, 1)
                dt_proj(s, 2)
                for m in range(MC):
                    if not over(s + 1) and m in XT_TURNS:
                        turn_xt(s + 1, XT_TURNS.index(m))
                    if m + 3 < MC:
                        dt_proj(s, m + 3)
                    out_proj(s, m)
            each(pe, body)


def kernel(**inputs):
    import numpy as np
    import concourse.bacc as bacc
    from concourse import mybir as m
    from concourse.bass_utils import run_bass_kernel_spmd

    a = {name.removeprefix("L0_"): np.asarray(value) for name, value in inputs.items()}

    def rows_on_partitions(w):
        return np.ascontiguousarray(w.reshape(-1, P, w.shape[1]).transpose(1, 0, 2))

    E, inner, D = a["ffn_w_gate"].shape
    R = a["attn_W_dt"].shape[1]
    gate_up = np.stack([a["ffn_w_gate"], a["ffn_w_up"]], 1)
    gate_up = gate_up.reshape(E, 2, inner, D // P, P).transpose(0, 4, 1, 3, 2).reshape(E, P, -1)
    down = a["ffn_w_down"].reshape(E, D, inner // P, P).transpose(0, 3, 2, 1).reshape(E, P, -1)
    arrays = {
        "x": a["attn_x"],
        "moe_w": np.ascontiguousarray(np.concatenate([gate_up, down], 2)),
        "gate_t": rows_on_partitions(a["ffn_gate_w"].T),
        "w_in": rows_on_partitions(a["attn_W_in"].T),
        "w_out": rows_on_partitions(a["attn_W_out"].T),
        "w_x": rows_on_partitions(a["attn_W_x"][:R].T),
        "w_dt": np.ascontiguousarray(a["attn_W_dt"].T),
        "conv_w": rows_on_partitions(a["attn_conv_w"][:, 0, :]),
        "conv_b": np.ascontiguousarray(a["attn_conv_b"].reshape(-1, P).T),
        "b_dt": np.ascontiguousarray(a["attn_b_dt"].reshape(-1, P).T),
    }
    nc = bacc.Bacc("TRN2", target_bir_lowering=False, num_devices=1)
    aps = {name: nc.dram_tensor(name, v.shape, m.dt.from_np(v.dtype), kind="ExternalInput").ap()
           for name, v in arrays.items()}
    shape = arrays["x"].shape
    out = nc.dram_tensor("out", shape, m.dt.float32, kind="ExternalOutput").ap()
    build_program(nc, out=out, **aps)
    result = run_bass_kernel_spmd(nc, [arrays], core_ids=[0])
    return result.results[0]["out"]
```

```python
from contextlib import ExitStack

import concourse.bass as bass
from concourse import mybir

F32 = mybir.dt.float32
F32R = mybir.dt.float32r
BF16 = mybir.dt.bfloat16
I32 = mybir.dt.int32
U8 = mybir.dt.uint8
ALU = mybir.AluOpType
ACT = mybir.ActivationFunctionType
AX = mybir.AxisListType

P = 128
GT = 4
GW = GT * P
TOP_K = 8
CAP = 128
EPS = 1e-5
NEG = -3.0e38
WIN = 8
SOFTPLUS_CAP = 40.0


def wait(eng, sem, value):
    if not isinstance(value, int) or value > 0:
        eng.wait_ge(sem, value)


def run_passes(eng, n, body):
    body(0)
    if n > 2:
        with eng.Fori(1, n - 1) as i:
            body(i)
    if n > 1:
        body(n - 1)


def known(step):
    return isinstance(step, int)


def row_stats(dve, src, stats, mv):
    for j in range(GT):
        dve.bn_stats(stats[:, j, :], src[:, j, :])
    dve.drain()
    for j in range(GT):
        dve.bn_aggr(mv[:, j, 0:2], stats[:, j, :])
    dve.drain()
    return dve.tensor_scalar(mv[:, :, 2], mv[:, :, 1], EPS, None, ALU.add)


def rstd_of(pool, mv, minus_half, rstd):
    return pool.tensor_tensor(rstd[:, :], mv[:, :, 2], minus_half[:, :], ALU.pow)


def normalise(dve, src, xn, mv, rstd):
    for j in range(GT):
        last = dve.tensor_scalar(xn[:, j, :], src[:, j, :], mv[:, j, 0:1], rstd[:, j:j + 1],
                                 ALU.subtract, ALU.mult)
    return last


class Router:

    def __init__(self, sb, tag, E):
        self.logits = sb(tag + "logits", [P, GT, E], F32)
        self.top8 = sb(tag + "top8", [P, GT, TOP_K], F32)
        self.rest = sb(tag + "rest", [P, GT, E], F32)
        self.shifted = sb(tag + "shifted", [P, GT, E], F32)
        self.expd = sb(tag + "expd", [P, GT, E], F32)
        self.mask = sb(tag + "mask", [P, GT, E], F32)
        self.chosen = sb(tag + "chosen", [P, GT, E], BF16)
        self.total = sb(tag + "total", [P, GT], F32)
        self.table = sb(tag + "table", [P, GT, E + 2], F32)

    @staticmethod
    def flat(t):
        return t[:, :, :].rearrange("p j e -> p (j e)")

    def pick(self, dve, E):
        for j in range(GT):
            dve.max(self.top8[:, j, :], self.logits[:, j, :])
        dve.drain()
        for j in range(GT):
            dve.match_replace(self.rest[:, j, :], self.top8[:, j, :], self.logits[:, j, :], NEG)
        dve.tensor_tensor(self.shifted[:, :, :], self.logits[:, :, :],
                          self.top8[:, :, 0:1].broadcast_to([P, GT, E]), ALU.subtract)
        dve.drain()
        dve.tensor_tensor(self.mask[:, :, :], self.logits[:, :, :], self.rest[:, :, :], ALU.not_equal)
        return dve.tensor_tensor(self.chosen[:, :, :], self.logits[:, :, :], self.rest[:, :, :],
                                 ALU.not_equal)

    def keep_stats(self, dve, E, mv, rstd):
        dve.tensor_copy(self.table[:, :, E], mv[:, :, 0])
        dve.tensor_copy(self.table[:, :, E + 1], rstd[:, :])

    def weigh(self, dve, E):
        dve.tensor_tensor(self.expd[:, :, :], self.expd[:, :, :], self.mask[:, :, :], ALU.mult)
        dve.drain()
        dve.tensor_reduce(self.total[:, :], self.expd[:, :, :], AX.X, ALU.add)
        dve.drain()
        dve.reciprocal(self.total[:, :], self.total[:, :])
        dve.drain()
        return dve.scalar_tensor_tensor(
            out=self.table[:, :, 0:E], in0=self.expd[:, :, :], scalar=0.5,
            in1=self.total[:, :].rearrange("p (j a) -> p j a", a=1).broadcast_to([P, GT, E]),
            op0=ALU.mult, op1=ALU.mult)


def build_program(nc, x, moe_w, gate_t, w_in, w_out, w_x, w_dt, conv_w, conv_b, b_dt, out):
    B, L, D = x.shape
    T = B * L
    E = gate_t.shape[2]
    KD = D // P
    MC = w_out.shape[1]
    DI = MC * P
    R = w_dt.shape[0]
    IN = (moe_w.shape[2] // (2 * KD + D // P)) if D == 512 else 0
    KI = IN // P
    NG = L // GW
    STEPS = B * NG
    TAPS = conv_w.shape[2]
    PAST = TAPS - 1
    assert B == 2 and E == 64 and 4 * R == P and GT * E <= 512 and D == 512
    assert moe_w.shape[2] == 2 * KD * IN + KI * D

    x_rows = x.rearrange("b l d -> (b l) d")
    out_rows = out.rearrange("b l d -> (b l) d")
    x1 = nc.dram_tensor("x1", [T, D], F32, kind="Internal").ap()
    x2 = nc.dram_tensor("x2", [T, D], F32, kind="Internal").ap()
    tab1 = nc.dram_tensor("tab1", [T, E + 2], F32, kind="Internal").ap()
    tab2 = nc.dram_tensor("tab2", [T, E + 2], F32, kind="Internal").ap()

    def group(rows, b, i):
        g = rows.rearrange("(b g j p) n -> b g p j n", b=B, j=GT, p=P)
        if known(i):
            return g[b, i]
        return g[b, bass.ds(i, 1)].rearrange("g p j n -> p (g j) n")

    with ExitStack() as top:
        def top_sb(name, shape, dt):
            return top.enter_context(nc.sbuf_tensor(name, shape, dt))

        ident = top_sb("ident", [P, P], F32)
        minus_half = top_sb("minus_half", [P, GT], F32)
        win_bits = top_sb("win_bits", [P, P // WIN], BF16)
        gate_sb = top_sb("gate_sb", [P, KD, E], F32)
        windows = top_sb("windows", [P, L // WIN], F32)
        slot_token = top_sb("slot_token", [P, E], I32)

        constants(nc, ident, win_bits, minus_half, gate_sb, gate_t)
        first_routing(nc, top, x_rows, x1, tab1, group, NG, KD, E, D, ident, win_bits, minus_half, gate_sb, windows)
        find_slots(nc, T, L, E, ident, windows, slot_token, "a")
        experts(nc, x_rows, tab1, x1, moe_w, T, E, D, KD, IN, KI, ident, slot_token, "a")
        mixer(nc, x1, x2, out_rows, tab2, group, NG, KD, MC, R, PAST, E, D, L, w_in, w_out, w_x, w_dt,
              conv_w, conv_b, b_dt, ident, win_bits, minus_half, gate_sb, windows)
        find_slots(nc, T, L, E, ident, windows, slot_token, "b")
        experts(nc, x2, tab2, out_rows, moe_w, T, E, D, KD, IN, KI, ident, slot_token, "b")


def constants(nc, ident, win_bits, minus_half, gate_sb, gate_t):
    with ExitStack() as ctx:
        made = ctx.enter_context(nc.semaphore("ident_made"))
        loaded = ctx.enter_context(nc.semaphore("gate_loaded"))
        block = ctx.enter_context(nc.Block())

        @block.gpsimd
        def _(pool):
            pool.memset(ident[:, :], 0.0).then_inc(made, 1)
            pool.memset(win_bits[:, :], 0.0).then_inc(made, 1)
            pool.wait_ge(made, 2)
            pool.affine_select(out=ident[:, :], in_=ident[:, :], compare_op=ALU.not_equal, fill=1.0,
                               base=0, pattern=[[-1, P]], channel_multiplier=1).then_inc(made, 1)
            pool.memset(minus_half[:, :], -0.5).then_inc(made, 1)
            for t in range(WIN):
                pool.wait_ge(made, 4 + t)
                pool.affine_select(out=win_bits[:, :], in_=win_bits[:, :], compare_op=ALU.not_equal,
                                   fill=float(2 ** (WIN - 1 - t)), base=-t,
                                   pattern=[[-WIN, P // WIN]], channel_multiplier=1).then_inc(made, 1)
            pool.wait_ge(made, 4 + WIN)

        @block.sync
        def _(sp):
            sp.dma_start(gate_sb[:, :, :], gate_t).then_inc(loaded, 16)
            sp.wait_ge(loaded, 16)


def first_routing(nc, top, x_rows, x1, tab1, group, NG, KD, E, D, ident, win_bits, minus_half, gate_sb, windows):
    STEPS = 2 * NG
    with ExitStack() as ctx:
        def sb(name, shape, dt):
            return ctx.enter_context(nc.sbuf_tensor("r_" + name, shape, dt))

        def psum(name):
            return ctx.enter_context(nc.psum_tensor("r_" + name, [P, 512], F32))

        def sem(name):
            return ctx.enter_context(nc.semaphore("r_" + name))

        X = [sb(f"x{b}", [P, GT, D], F32) for b in range(2)]
        XN = [sb(f"xn{b}", [P, GT, D], F32) for b in range(2)]
        XT = [sb(f"xt{b}", [P, KD, GW], F32) for b in range(2)]
        stats = sb("stats", [P, GT, 6], F32)
        mv = [sb(f"mv{b}", [P, GT, 3], F32) for b in range(2)]
        neg_mean = [sb(f"neg_mean{b}", [P, GT], F32) for b in range(2)]
        rstd = [sb(f"rstd{b}", [P, GT], F32) for b in range(2)]
        shift = [sb(f"shift{b}", [P, GT], F32) for b in range(2)]
        rt = [Router(sb, f"rt{b}_", E) for b in range(2)]
        turn_ps = [psum(f"turn{n}") for n in range(2)]
        logit_ps = [psum(f"logit{b}") for b in range(2)]
        chosen_ps = [psum(f"chosen{b}") for b in range(2)]

        x_in = [sem(f"x_in{b}") for b in range(2)]
        x1_out = [sem(f"x1_out{b}") for b in range(2)]
        var_made = sem("var_made")
        rstd_made = sem("rstd_made")
        shift_made = sem("shift_made")
        xn_made = sem("xn_made")
        turned = sem("turned")
        xt_made = sem("xt_made")
        logits_done = sem("logits_done")
        logits_read = sem("logits_read")
        chosen_made = sem("chosen_made")
        exp_made = sem("exp_made")
        chosen_turned = sem("chosen_turned")
        table_made = sem("table_made")
        table_out = [sem(f"table_out{b}") for b in range(2)]
        block = ctx.enter_context(nc.Block())

        def each(eng, body):
            def one_pass(i):
                for b in range(2):
                    body(i * 2 + b, i, b)
            run_passes(eng, NG, one_pass)
            one_pass(NG)

        def early(s):
            return known(s) and s < 2

        def over(s):
            return known(s) and s >= STEPS

        @block.sync
        def _(sp):
            for b in range(2):
                sp.dma_start(X[b][:, :, :], group(x_rows, b, 0)).then_inc(x_in[b], 16)

            def one_pass(i):
                for b in range(2):
                    sp.wait_ge(x_in[b], i * 16 + 16)
                    sp.dma_start(group(x1, b, i), X[b][:, :, :]).then_inc(x1_out[b], 16)
                if known(i) and i == NG - 1:
                    return
                for b in range(2):
                    sp.wait_ge(xn_made, (i * 2 + b + 1) * GT)
                    sp.wait_ge(x1_out[b], i * 16 + 16)
                    sp.dma_start(X[b][:, :, :], group(x_rows, b, i + 1)).then_inc(x_in[b], 16)
            run_passes(sp, NG, one_pass)
            for b in range(2):
                sp.wait_ge(x1_out[b], 16 * NG)

        @block.vector
        def _(dve):
            def body(s, i, b):
                r = rt[b]
                if not early(s):
                    dve.wait_ge(logits_done, s - 1)
                    dve.tensor_copy(r.flat(r.logits), logit_ps[b][:, 0:GT * E])\
                       .then_inc(logits_read, 1)
                    dve.drain()
                    wait(dve, table_out[b], (i - 1) * 16)
                    r.keep_stats(dve, E, mv[b], rstd[b])
                    r.pick(dve, E).then_inc(chosen_made, 1)
                if not over(s):
                    dve.wait_ge(x_in[b], i * 16 + 16)
                    row_stats(dve, X[b], stats, mv[b])
                    dve.tensor_scalar(neg_mean[b][:, :], mv[b][:, :, 0], -1.0, None, ALU.mult)\
                       .then_inc(var_made, 1)
                    dve.drain()
                if not early(s):
                    dve.wait_ge(exp_made, s - 1)
                    r.weigh(dve, E).then_inc(table_made, 1)
                    dve.wait_ge(chosen_turned, s - 1)
                    h = slice(64 * b, 64 * b + 64)
                    dve.tensor_copy(windows[h, bass.ds((i - 1) * (GW // WIN), GW // WIN)],
                                    chosen_ps[b][h, 0:GW // WIN])
            each(dve, body)

        @block.scalar
        def _(act):
            def body(s, i, b):
                if not early(s):
                    act.wait_ge(chosen_made, s - 1)
                    act.activation(rt[b].flat(rt[b].expd), rt[b].flat(rt[b].shifted), ACT.Exp)\
                       .then_inc(exp_made, 1)
                if over(s):
                    return
                act.wait_ge(shift_made, s + 1)
                for j in range(GT + 1):
                    if j < GT:
                        act.activation(XN[b][:, j, :], X[b][:, j, :], ACT.Identity,
                                       bias=shift[b][:, j:j + 1], scale=rstd[b][:, j:j + 1])\
                           .then_inc(xn_made, 1)
                    if j >= 1:
                        t = j - 1
                        act.wait_ge(turned, s * GT + t + 1)
                        act.activation(XT[b][:, :, t * P:(t + 1) * P],
                                       turn_ps[t % 2][:, :].rearrange("p (k t) -> p k t", k=KD),
                                       ACT.Copy).then_inc(xt_made, 1)
            each(act, body)

        @block.tensor
        def _(pe):
            def body(s, i, b):
                if not early(s):
                    pe.wait_ge(chosen_made, s - 1)
                    turn_mask(pe, chosen_ps[b], rt[b], win_bits, b).then_inc(chosen_turned, 1)
                if over(s):
                    return
                for j in range(GT + 1):
                    if j < GT:
                        pe.wait_ge(xn_made, s * GT + j + 1)
                        wait(pe, xt_made, s * GT + j - 1)
                        for k in range(KD):
                            mm = pe.transpose(turn_ps[j % 2][:, k * P:(k + 1) * P],
                                              XN[b][:, j, k * P:(k + 1) * P], ident[:, :])
                        mm.then_inc(turned, 1)
                    if j == 1 and not early(s):
                        pe.wait_ge(logits_read, s - 1)
                    if j >= 1:
                        pe.wait_ge(xt_made, s * GT + j)
                        mm = tile_logits(pe, logit_ps[b], XT[b], gate_sb, KD, E, j - 1)
                mm.then_inc(logits_done, 1)
            each(pe, body)

        @block.gpsimd
        def _(pool):
            def body(s, i, b):
                if not over(s):
                    pool.wait_ge(var_made, s + 1)
                    rstd_of(pool, mv[b], minus_half, rstd[b]).then_inc(rstd_made, 1)
                    pool.wait_ge(rstd_made, s + 1)
                    pool.tensor_tensor(shift[b][:, :], neg_mean[b][:, :], rstd[b][:, :], ALU.mult)\
                        .then_inc(shift_made, 1)
                if not early(s):
                    pool.wait_ge(table_made, s - 1)
                    pool.dma_start(group(tab1, b, i - 1), rt[b].table[:, :, :])\
                        .then_inc(table_out[b], 16)
            each(pool, body)
            for b in range(2):
                pool.wait_ge(table_out[b], 16 * NG)


def logits(pe, bank, xt, gate_sb, KD, E):
    for j in range(GT):
        mm = tile_logits(pe, bank, xt, gate_sb, KD, E, j)
    return mm


def tile_logits(pe, bank, xt, gate_sb, KD, E, j):
    for k in range(KD):
        mm = pe.matmul(bank[:, j * E:(j + 1) * E], xt[:, k, j * P:(j + 1) * P], gate_sb[:, k, :],
                       start=(k == 0), stop=(k == KD - 1))
    return mm


def turn_mask(pe, bank, router, win_bits, b):
    n = P // WIN
    for j in range(GT):
        mm = pe.matmul(bank[64 * b:64 * b + 64, j * n:(j + 1) * n], router.chosen[:, j, :],
                       win_bits[:, :], start=True, stop=True)
    return mm


def find_slots(nc, T, L, E, ident, windows, slot_token, tag):
    LW, NW = L // WIN, T // WIN
    bits = 2 ** WIN
    flag = 2 * bits * NW
    assert LW >= CAP and 2 * flag <= 2 ** 24 and NW & (NW - 1) == 0
    with ExitStack() as ctx:
        def sb(name, shape, dt):
            return ctx.enter_context(nc.sbuf_tensor(f"f{tag}_{name}", shape, dt))

        def sem(name):
            return ctx.enter_context(nc.semaphore(f"f{tag}_{name}"))

        number = sb("number", [P, LW], I32)
        back = sb("back", [P, WIN], I32)
        flags = sb("flags", [P, LW], F32)
        win_keys = sb("win_keys", [P, LW], F32)
        best_win = sb("best_win", [P, CAP], F32)
        packed = sb("packed", [P, CAP], I32)
        first = sb("first", [P, CAP], I32)
        bit = sb("bit", [P, CAP, WIN], I32)
        keys = sb("keys", [P, CAP, WIN], F32)
        best = sb("best", [P, CAP], F32)
        both = sb("both", [E, 2 * CAP], F32)
        final = sb("final", [E, CAP], F32)
        raised = sb("raised", [P, E], F32)
        turned_ps = ctx.enter_context(nc.psum_tensor(f"f{tag}_turned", [P, E], F32))
        numbered = sem("numbered")
        final_made = sem("final_made")
        final_turned = sem("final_turned")
        block = ctx.enter_context(nc.Block())

        @block.gpsimd
        def _(pool):
            for b in range(2):
                pool.iota(number[64 * b:64 * b + 64, :], [[-bits, LW]], base=bits * (NW - b * LW),
                          channel_multiplier=0).then_inc(numbered, 1)
            pool.wait_ge(numbered, 2)
            pool.iota(back[:, :], [[-1, WIN]], base=0, channel_multiplier=0).then_inc(numbered, 1)

        @block.vector
        def _(dve):
            def take(keys, best, n):
                for r in range(n // TOP_K):
                    eight = best[:, r * TOP_K:(r + 1) * TOP_K]
                    dve.max(eight, keys)
                    dve.drain()
                    dve.match_replace(keys, eight, keys, 0.0)
                    dve.drain()

            dve.tensor_scalar(flags[:, :], windows[:, :], 0.0, float(flag), ALU.is_gt, ALU.mult)
            dve.wait_ge(numbered, 3)
            dve.scalar_tensor_tensor(out=win_keys[:, :], in0=windows[:, :], scalar=1.0,
                                     in1=number[:, :], op0=ALU.mult, op1=ALU.add)
            dve.drain()
            dve.tensor_tensor(win_keys[:, :], win_keys[:, :], flags[:, :], ALU.add)
            dve.drain()
            take(win_keys[:, :], best_win[:, :], CAP)
            dve.tensor_copy(packed[:, :], best_win[:, :])
            dve.drain()
            shift = WIN - (WIN.bit_length() - 1)
            dve.tensor_scalar(first[:, :], packed[:, :], shift, 2 * T - WIN,
                              ALU.logical_shift_right, ALU.bitwise_and)
            for t in range(WIN):
                dve.tensor_scalar(bit[:, :, t], packed[:, :], WIN - 1 - t, 1,
                                  ALU.logical_shift_right, ALU.bitwise_and)
            dve.drain()
            for t in range(WIN):
                dve.scalar_tensor_tensor(out=keys[:, :, t], in0=bit[:, :, t], scalar=float(T),
                                         in1=first[:, :], op0=ALU.mult, op1=ALU.add)
            dve.drain()
            dve.tensor_tensor(keys[:, :, :], keys[:, :, :],
                              back[:, :].rearrange("p (a t) -> p a t", a=1)
                              .broadcast_to([P, CAP, WIN]), ALU.add)
            dve.drain()
            take(keys[:, :, :].rearrange("p c t -> p (c t)"), best[:, :], CAP)
            for b in range(2):
                dve.tensor_copy(both[:, b * CAP:(b + 1) * CAP], best[64 * b:64 * b + 64, :])
            dve.drain()
            take(both[:, :], final[:, :], CAP)
            dve.drain().then_inc(final_made, 1)
            dve.wait_ge(final_turned, 1)
            dve.tensor_scalar(raised[:, :], turned_ps[:, :], float(T), float(T), ALU.is_gt, ALU.mult)
            dve.drain()
            dve.tensor_tensor(raised[:, :], raised[:, :], turned_ps[:, :], ALU.subtract)
            dve.drain()
            dve.tensor_scalar(slot_token[:, :], raised[:, :], float(T), None, ALU.add)

        @block.tensor
        def _(pe):
            pe.wait_ge(final_made, 1)
            pe.transpose(turned_ps[:, :], final[:, :], ident[0:E, 0:E]).then_inc(final_turned, 1)


def experts(nc, src, table, dst, moe_w, T, E, D, KD, IN, KI, ident, slot_token, tag):
    RING = 4
    EW = moe_w.shape[2]
    GU = KD * IN
    with ExitStack() as ctx:
        def sb(name, shape, dt):
            return ctx.enter_context(nc.sbuf_tensor(f"m{tag}_{name}", shape, dt))

        def psum(name, n):
            return ctx.enter_context(nc.psum_tensor(f"m{tag}_{name}", [P, n], F32))

        def sem(name):
            return ctx.enter_context(nc.semaphore(f"m{tag}_{name}"))

        W = [sb(f"w{k}", [P, EW], F32) for k in range(RING)]
        XG = [sb(f"xg{k}", [P, D], F32) for k in range(RING)]
        tab = [sb(f"tab{k}", [P, E + 2], F32) for k in range(RING)]
        fetched = [sb(f"fetched{k}", [P, 1], I32) for k in range(RING)]
        stored = [sb(f"stored{k}", [P, 1], I32) for k in range(RING)]
        zero = sb("zero", [P, 1], F32)
        mark = sb("mark", [P, 2 * RING], F32)
        XN = [sb(f"xn{k}", [P, D], F32) for k in range(2)]
        XT = [sb(f"xt{k}", [P, KD, P], F32) for k in range(2)]
        act_g = [sb(f"act_g{k}", [P, IN], F32) for k in range(2)]
        gu = [sb(f"gu{k}", [P, IN], F32) for k in range(2)]
        guT = [sb(f"guT{k}", [P, KI, P], F32) for k in range(2)]
        result = [sb(f"result{k}", [P, D], F32) for k in range(2)]
        x_ps = psum("x", D)
        gate_ps = psum("gate", IN)
        up_ps = psum("up", IN)
        gu_ps = psum("gu", IN)
        down_ps = [psum(f"down{k}", D) for k in range(2)]

        gate_in = [sem(f"gate_in{k}") for k in range(RING)]
        up_in = [sem(f"up_in{k}") for k in range(RING)]
        down_in = [sem(f"down_in{k}") for k in range(RING)]
        zeroed = sem("zeroed")
        held = sem("held")
        indexed = sem("indexed")
        stored_made = sem("stored_made")
        rows_in = [sem(f"rows_in{k}") for k in range(RING)]
        tab_in = [sem(f"tab_in{k}") for k in range(RING)]
        added = sem("added")
        xn_made = sem("xn_made")
        x_turned = sem("x_turned")
        xt_made = sem("xt_made")
        gate_done = sem("gate_done")
        up_done = sem("up_done")
        act_made = sem("act_made")
        gu_made = sem("gu_made")
        gu_turned = sem("gu_turned")
        guT_made = sem("guT_made")
        down_done = sem("down_done")
        result_made = sem("result_made")
        block = ctx.enter_context(nc.Block())

        def each(eng, body):
            def one_pass(i):
                for k in range(RING):
                    body(i, k, i * RING + k)
            run_passes(eng, E // RING, one_pass)

        def beyond(e):
            return known(e) and e >= E

        @block.sync
        def _(sp):
            def part(e, at, n):
                rows = moe_w[e] if known(e) else moe_w[bass.ds(e, 1)].rearrange("a p n -> p (a n)")
                return rows[:, at:at + n]

            def body(i, k, e):
                for at, n, done, landed in ((0, GU, gate_done, gate_in), (GU, GU, up_done, up_in),
                                            (2 * GU, KI * D, down_done, down_in)):
                    wait(sp, done, e - RING + 1)
                    sp.dma_start(W[k][:, at:at + n], part(e, at, n)).then_inc(landed[k], 16)
            each(sp, body)

        @block.gpsimd
        def _(pool):
            def hold(e, k, which):
                wait(pool, held, 2 * (e - RING) + which + 1)
                at = slice(2 * k + which, 2 * k + which + 1)
                pool.tensor_tensor(mark[:, at], zero[:, :], zero[:, :], ALU.add).then_inc(held, 1)

            def fetch(e, k):
                wait(pool, xn_made, e - RING + 1)
                pool.tensor_copy(fetched[k][:, :], slot_token[:, bass.ds(e, 1)]).then_inc(indexed, 1)
                pool.wait_ge(indexed, e + 1)
                hold(e, k, 0)
                for rows, there, landed in ((XG[k], src, rows_in[k]), (tab[k], table, tab_in[k])):
                    pool.indirect_dma_start(
                        out=rows[:, :], out_offset=None, in_=there,
                        in_offset=bass.IndirectOffsetOnAxis(ap=fetched[k][:, :], axis=0))\
                        .then_inc(landed, 16)

            pool.memset(zero[:, :], 0.0).then_inc(zeroed, 1)
            pool.wait_ge(zeroed, 1)
            for e in range(RING - 1):
                fetch(e, e)

            def body(i, k, e):
                pool.tensor_copy(stored[k][:, :], slot_token[:, bass.ds(e, 1)]).then_inc(stored_made, 1)
                if not beyond(e + RING - 1):
                    fetch(e + RING - 1, (k + RING - 1) % RING)
                pool.wait_ge(stored_made, e + 1)
                wait(pool, added, e * 16)
                pool.wait_ge(result_made, e + 1)
                hold(e, k, 1)
                pool.indirect_dma_start(
                    out=dst, out_offset=bass.IndirectOffsetOnAxis(ap=stored[k][:, :], axis=0),
                    in_=result[k % 2][:, :], in_offset=None, compute_op=ALU.add).then_inc(added, 16)
            each(pool, body)
            pool.wait_ge(added, 16 * E)

        @block.vector
        def _(dve):
            def norm(i, e, k):
                dve.wait_ge(rows_in[k], i * 16 + 16)
                wait(dve, x_turned, e - 1)
                dve.wait_ge(tab_in[k], i * 16 + 16)
                dve.tensor_scalar(XN[k % 2][:, :], XG[k][:, :], tab[k][:, E:E + 1],
                                  tab[k][:, E + 1:E + 2], ALU.subtract, ALU.mult).then_inc(xn_made, 1)

            def mul(e, k):
                dve.wait_ge(act_made, e + 1)
                dve.wait_ge(up_done, e + 1)
                dve.tensor_tensor(gu[k % 2][:, :], act_g[k % 2][:, :], up_ps[:, :], ALU.mult)\
                   .then_inc(gu_made, 1)

            norm(0, 0, 0)
            norm(0, 1, 1)
            mul(0, 0)

            def body(i, k, e):
                if not beyond(e + 2):
                    norm(i + (k + 2) // RING, e + 2, (k + 2) % RING)
                if not beyond(e + 1):
                    mul(e + 1, k + 1)
                dve.wait_ge(down_done, e + 1)
                wait(dve, added, (e - 1) * 16)
                dve.tensor_scalar(result[k % 2][:, :], down_ps[k % 2][:, :],
                                  tab[k][:, bass.ds(e, 1)], None, ALU.mult).then_inc(result_made, 1)
            each(dve, body)

        @block.scalar
        def _(act):
            def copy_xt(e, k):
                act.wait_ge(x_turned, e + 1)
                act.activation(XT[k % 2][:, :, :].rearrange("p k c -> p (k c)"), x_ps[:, :], ACT.Copy)\
                   .then_inc(xt_made, 1)

            def silu(e, k):
                act.wait_ge(gate_done, e + 1)
                act.activation(act_g[k % 2][:, :], gate_ps[:, :], ACT.Silu).then_inc(act_made, 1)

            copy_xt(0, 0)
            silu(0, 0)
            copy_xt(1, 1)

            def body(i, k, e):
                if not beyond(e + 1):
                    silu(e + 1, k + 1)
                act.wait_ge(gu_turned, e + 1)
                act.activation(guT[k % 2][:, :, :].rearrange("p k c -> p (k c)"), gu_ps[:, :], ACT.Copy)\
                   .then_inc(guT_made, 1)
                if not beyond(e + 2):
                    copy_xt(e + 2, k)
            each(act, body)

        @block.tensor
        def _(pe):
            def turn_x(e, k):
                pe.wait_ge(xn_made, e + 1)
                for c in range(KD):
                    mm = pe.transpose(x_ps[:, c * P:(c + 1) * P], XN[k % 2][:, c * P:(c + 1) * P],
                                      ident[:, :])
                mm.then_inc(x_turned, 1)

            def project(bank, k, part):
                w = W[k % RING]
                for c in range(KD):
                    at = part * GU + c * IN
                    mm = pe.matmul(bank[:, :], XT[k % 2][:, c, :], w[:, at:at + IN],
                                   start=(c == 0), stop=(c == KD - 1))
                return mm

            def gate(i, e, k):
                pe.wait_ge(gate_in[k % RING], i * 16 + 16)
                pe.wait_ge(xt_made, e + 1)
                wait(pe, act_made, e)
                project(gate_ps, k, 0).then_inc(gate_done, 1)

            def up(i, e, k):
                pe.wait_ge(up_in[k % RING], i * 16 + 16)
                project(up_ps, k, 1).then_inc(up_done, 1)

            turn_x(0, 0)
            gate(0, 0, 0)
            up(0, 0, 0)
            turn_x(1, 1)

            def body(i, k, e):
                if not beyond(e + 1):
                    gate(i + (k + 1) // RING, e + 1, k + 1)
                pe.wait_ge(gu_made, e + 1)
                for c in range(KI):
                    mm = pe.transpose(gu_ps[:, c * P:(c + 1) * P], gu[k % 2][:, c * P:(c + 1) * P],
                                      ident[:, :])
                mm.then_inc(gu_turned, 1)
                if not beyond(e + 1):
                    up(i + (k + 1) // RING, e + 1, k + 1)
                if not beyond(e + 2):
                    turn_x(e + 2, k)
                pe.wait_ge(guT_made, e + 1)
                pe.wait_ge(down_in[k], i * 16 + 16)
                wait(pe, result_made, e - 1)
                for c in range(KI):
                    at = 2 * GU + c * D
                    mm = pe.matmul(down_ps[k % 2][:, :], guT[k % 2][:, c, :], W[k][:, at:at + D],
                                   start=(c == 0), stop=(c == KI - 1))
                mm.then_inc(down_done, 1)
            each(pe, body)


def mixer(nc, x1, x2, out_rows, tab2, group, NG, KD, MC, R, PAST, E, D, L, w_in, w_out, w_x, w_dt,
          conv_w, conv_b, b_dt, ident, win_bits, minus_half, gate_sb, windows):
    STEPS = 2 * NG
    DI = MC * P
    XT_TURNS = (0, 2, 4, 5)
    assert len(XT_TURNS) == KD
    with ExitStack() as ctx:
        def sb(name, shape, dt):
            return ctx.enter_context(nc.sbuf_tensor("c_" + name, shape, dt))

        def psum(name):
            return ctx.enter_context(nc.psum_tensor("c_" + name, [P, GW], F32))

        def sem(name):
            return ctx.enter_context(nc.semaphore("c_" + name))

        w_in_hi = sb("w_in_hi", [P, KD, 2 * DI], F32R)
        w_in_lo = sb("w_in_lo", [P, KD, 2 * DI], F32R)
        w_out_hi = sb("w_out_hi", [P, MC, D], F32R)
        w_out_lo = sb("w_out_lo", [P, MC, D], F32R)
        w_x_hi = sb("w_x_hi", [P, MC, P], F32R)
        w_x_lo = sb("w_x_lo", [P, MC, P], F32R)
        w_dt_parts = sb("w_dt_parts", [P, DI], F32R)
        taps = sb("taps", [P, MC, PAST + 1], F32)
        conv_bias = sb("conv_bias", [P, MC], F32)
        dt_bias = sb("dt_bias", [P, MC], F32)
        X = [sb(f"x{b}", [P, GT, D], F32) for b in range(2)]
        XN = sb("xn", [P, GT, D], F32)
        xt_hi = sb("xt_hi", [P, KD, GW], F32R)
        xt_lo = sb("xt_lo", [P, KD, GW], F32R)
        x2t = sb("x2t", [P, KD, GW], F32)
        gated = sb("gated", [P, MC, GW], F32)
        half_hi = [sb(f"half_hi{k}", [P, GW], F32R) for k in range(2)]
        half_lo = [sb(f"half_lo{k}", [P, GW], F32R) for k in range(2)]
        xs = [sb(f"xs{k}", [P, PAST + GW], F32) for k in range(2)]
        temp = [sb(f"temp{k}", [P, GW], F32) for k in range(2)]
        silu_z = [sb(f"silu_z{k}", [P, GW], F32) for k in range(2)]
        chain = temp + silu_z
        dt_parts = sb("dt_parts", [P, GW], F32R)
        past = [sb(f"past{b}", [P, MC, PAST], F32) for b in range(2)]
        stats = sb("stats", [P, GT, 6], F32)
        mv, mv2 = (sb(f"mv{n}", [P, GT, 3], F32) for n in (1, 2))
        rstd, rstd2 = (sb(f"rstd{n}", [P, GT], F32) for n in (1, 2))
        router = Router(sb, "rt_", E)

        with ExitStack() as prep:
            landed = [prep.enter_context(nc.semaphore(f"p_landed{k}")) for k in range(2)]
            small_in = prep.enter_context(nc.semaphore("p_small_in"))
            hi_made = prep.enter_context(nc.semaphore("p_hi_made"))
            lo_made = prep.enter_context(nc.semaphore("p_lo_made"))
            block = prep.enter_context(nc.Block())
            stage = [X[k][:, :, :].rearrange("p j d -> p (j d)") for k in range(2)]
            flat = "p k n -> p (k n)"
            half = MC // 2
            assert 2 * DI == GT * D and half * D == GT * D and MC * P <= GT * D and DI <= GT * D
            pieces = [(w_in[:, k, :], w_in_hi[:, k, :], w_in_lo[:, k, :]) for k in range(KD)]
            pieces += [(w_out[:, h * half:(h + 1) * half, :].rearrange(flat),
                        w_out_hi[:, h * half:(h + 1) * half, :].rearrange(flat),
                        w_out_lo[:, h * half:(h + 1) * half, :].rearrange(flat)) for h in range(2)]
            N = len(pieces)

            @block.sync
            def _(sp):
                for n, (src, _, _) in enumerate(pieces):
                    wait(sp, lo_made, n - 1)
                    sp.dma_start(stage[n % 2], src).then_inc(landed[n % 2], 16)
                sp.wait_ge(lo_made, N)
                for c in range(4):
                    dst = stage[0][:, 0:MC * P].rearrange("p (m c r) -> p m c r", m=MC, c=4)
                    sp.dma_start(dst[:, :, c, :], w_x).then_inc(landed[0], 16)
                    sp.dma_start(stage[1][c * R:(c + 1) * R, 0:DI], w_dt).then_inc(landed[1], 16)
                for dst, src in ((taps, conv_w), (conv_bias, conv_b), (dt_bias, b_dt)):
                    sp.dma_start(dst[:], src).then_inc(small_in, 16)
                sp.wait_ge(small_in, 48)

            def last_landed(eng):
                eng.wait_ge(landed[0], 16 * (N // 2 + 4))
                eng.wait_ge(landed[1], 16 * (N // 2 + 4))

            @block.scalar
            def _(act):
                for n, (_, hi, _) in enumerate(pieces):
                    act.wait_ge(landed[n % 2], 16 * (n // 2 + 1))
                    act.activation(hi, stage[n % 2], ACT.Copy).then_inc(hi_made, 1)
                last_landed(act)
                act.activation(w_x_hi[:, :, :].rearrange(flat), stage[0][:, 0:MC * P], ACT.Copy)\
                   .then_inc(hi_made, 1)
                act.activation(w_dt_parts[:, :], stage[1][:, 0:DI], ACT.Copy).then_inc(hi_made, 1)

            @block.vector
            def _(dve):
                for b in range(2):
                    dve.memset(past[b][:, :, :], 0.0)
                for n, (_, hi, lo) in enumerate(pieces):
                    dve.wait_ge(hi_made, n + 1)
                    dve.tensor_tensor(lo, stage[n % 2], hi, ALU.subtract).then_inc(lo_made, 1)
                dve.wait_ge(hi_made, N + 2)
                dve.tensor_tensor(w_x_lo[:, :, :].rearrange(flat), stage[0][:, 0:MC * P],
                                  w_x_hi[:, :, :].rearrange(flat), ALU.subtract)
                low = slice(2 * R, 4 * R)
                dve.tensor_tensor(w_dt_parts[low, :], stage[1][low, 0:DI], w_dt_parts[low, :],
                                  ALU.subtract)

        chunk_ps = [psum(f"chunk{k}") for k in range(2)]
        dt_ps = psum("dt")
        v_ps = [dt_ps] + chunk_ps
        turn_ps = psum("turn")
        out_ps = [psum(f"out{j}") for j in range(GT)]

        x_in = [sem(f"x_in{b}") for b in range(2)]
        var_made = sem("var_made")
        rstd_made = sem("rstd_made")
        xn_made = sem("xn_made")
        res_made = sem("res_made")
        turned = sem("turned")
        xt_hi_made = sem("xt_hi_made")
        xt_made = sem("xt_made")
        xs_done = sem("xs_done")
        xs_read = sem("xs_read")
        past_in = sem("past_in")
        conv_made = sem("conv_made")
        xc_hi_made = sem("xc_hi_made")
        xc_made = sem("xc_made")
        xp_done = sem("xp_done")
        dt_hi_made = sem("dt_hi_made")
        dt_made = sem("dt_made")
        z_done = sem("z_done")
        z_read = sem("z_read")
        gate_made = sem("gate_made")
        v_done = sem("v_done")
        v_capped = sem("v_capped")
        exp_done = sem("exp_done")
        log_done = sem("log_done")
        v_read = sem("v_read")
        y_made = sem("y_made")
        y_hi_made = sem("y_hi_made")
        y_parts_made = sem("y_parts_made")
        out_done = sem("out_done")
        x2_made = sem("x2_made")
        x2_out = [sem(f"x2_out{b}") for b in range(2)]
        var2_made = sem("var2_made")
        rstd2_made = sem("rstd2_made")
        xn2_made = sem("xn2_made")
        turned2 = sem("turned2")
        x2t_made = sem("x2t_made")
        logits_done = sem("logits_done")
        logits_read = sem("logits_read")
        chosen_made = sem("chosen_made")
        chosen_turned = sem("chosen_turned")
        chosen_read = sem("chosen_read")
        exps_made = sem("exps_made")
        table_made = sem("table_made")
        table_out = sem("table_out")
        block = ctx.enter_context(nc.Block())

        def each(eng, body):
            def one_pass(i):
                for b in range(2):
                    body(i * 2 + b, i, b)
            run_passes(eng, NG, one_pass)
            body(STEPS, NG, 0)

        def first(s):
            return known(s) and s == 0

        def over(s):
            return known(s) and s >= STEPS

        def before(i, b):
            return (i, 0) if b == 1 else (i - 1, 1)

        @block.sync
        def _(sp):
            sp.dma_start(X[0][:, :, :], group(x1, 0, 0)).then_inc(x_in[0], 16)
            sp.dma_start(X[1][:, :, :], group(x1, 1, 0)).then_inc(x_in[1], 16)

            def body(s, i, b):
                if not first(s):
                    pi, pb = before(i, b)
                    if not over(s + 1):
                        sp.wait_ge(xn2_made, s)
                        sp.wait_ge(x2_out[pb], pi * 32 + 32)
                        sp.dma_start(X[pb][:, :, :], group(x1, pb, pi + 1)).then_inc(x_in[pb], 16)
            each(sp, body)
            for b in range(2):
                sp.wait_ge(x2_out[b], 32 * NG)
            sp.wait_ge(table_out, 16 * STEPS)

        def norm1(dve, s, i, b):
            dve.wait_ge(x_in[b], i * 16 + 16)
            row_stats(dve, X[b], stats, mv).then_inc(var_made, 1)
            dve.drain()
            dve.wait_ge(rstd_made, s + 1)
            normalise(dve, X[b], XN, mv, rstd).then_inc(xn_made, 1)

        def low_xt(dve, s, k):
            dve.wait_ge(xt_hi_made, s * KD + k + 1)
            dve.tensor_tensor(xt_lo[:, k, :], turn_ps[:, :], xt_hi[:, k, :], ALU.subtract)\
               .then_inc(xt_made, 1)

        @block.vector
        def _(dve):
            norm1(dve, 0, 0, 0)
            for k in range(KD):
                low_xt(dve, 0, k)

            def take_past(c, m, b):
                wait(dve, conv_made, c - 1)
                dve.tensor_copy(xs[m % 2][:, 0:PAST], past[b][:, m, :]).then_inc(past_in, 1)

            def convolve(c, m, b):
                t = temp[m % 2][:, :]
                dve.wait_ge(xs_read, c + 1)
                dve.wait_ge(past_in, c + 1)
                for tap in range(PAST):
                    conv = dve.scalar_tensor_tensor(
                        out=t, in0=xs[m % 2][:, tap:tap + GW], scalar=taps[:, m, tap:tap + 1],
                        in1=t, op0=ALU.mult, op1=ALU.add)
                    if tap < PAST - 1:
                        dve.drain()
                conv.then_inc(conv_made, 1)
                if m + 2 < MC:
                    take_past(c + 2, m + 2, b)

            def cap(v, m):
                dve.wait_ge(v_done, v + 1)
                if m >= 4:
                    dve.wait_ge(y_made, v - 3)
                dve.tensor_scalar(chain[m % 4][:, :], v_ps[m % 3][:, :], dt_bias[:, m:m + 1],
                                  SOFTPLUS_CAP, ALU.add, ALU.min).then_inc(v_capped, 1)

            def softplus(v, m):
                t = chain[m % 4][:, :]
                dve.wait_ge(log_done, v + 1)
                dve.scalar_tensor_tensor(out=t, in0=v_ps[m % 3][:, :], scalar=dt_bias[:, m:m + 1],
                                         in1=t, op0=ALU.add, op1=ALU.max).then_inc(v_read, 1)
                dve.wait_ge(v_read, v + 1)
                dve.wait_ge(gate_made, v + 1)
                dve.tensor_tensor(gated[:, m, :], gated[:, m, :], t, ALU.mult).then_inc(y_made, 1)

            for m in range(2):
                take_past(m, m, 0)

            def body(s, i, b):
                pi, pb = before(i, b)
                if not first(s):
                    dve.wait_ge(out_done, s * MC)
                    for j in range(GT):
                        last = dve.tensor_tensor(X[pb][:, j, :], X[pb][:, j, :], out_ps[j][:, :], ALU.add)
                    last.then_inc(x2_made, 1)
                    dve.drain()
                    row_stats(dve, X[pb], stats, mv2).then_inc(var2_made, 1)
                if not over(s):
                    convolve(s * MC, 0, b)
                if not first(s):
                    if over(s):
                        dve.drain()
                    else:
                        wait(dve, turned, s * KD + KD)
                    dve.wait_ge(rstd2_made, s)
                    normalise(dve, X[pb], XN, mv2, rstd2).then_inc(xn2_made, 1)
                if not over(s):
                    for m in range(1, MC):
                        convolve(s * MC + m, m, b)
                if not first(s):
                    dve.wait_ge(logits_done, s)
                    dve.tensor_copy(router.flat(router.logits), turn_ps[:, 0:GT * E])\
                       .then_inc(logits_read, 1)
                    dve.drain()
                    router.pick(dve, E).then_inc(chosen_made, 1)
                if not over(s):
                    dve.wait_ge(dt_hi_made, s + 1)
                    for c in (1, 3):
                        rows = slice(c * R, (c + 1) * R)
                        low = dve.tensor_tensor(dt_parts[rows, :], dt_ps[rows, :], dt_parts[rows, :],
                                                ALU.subtract)
                    low.then_inc(dt_made, 1)
                nb = 1 - b
                if not over(s + 1):
                    if first(s):
                        dve.wait_ge(turned, KD)
                        dve.wait_ge(res_made, 1)
                    norm1(dve, s + 1, i + b, nb)
                if not first(s):
                    dve.wait_ge(chosen_turned, s)
                    h = slice(64 * pb, 64 * pb + 64)
                    dve.tensor_copy(windows[h, bass.ds(pi * (GW // WIN), GW // WIN)],
                                    turn_ps[h, 0:GW // WIN])\
                       .then_inc(chosen_read, 1)
                if not over(s):
                    v = s * MC
                    cap(v, 0)
                    cap(v + 1, 1)
                    dve.wait_ge(gate_made, v + MC)
                    cap(v + 2, 2)
                    for m in range(MC):
                        softplus(v + m, m)
                        if 3 <= m + 2 < MC:
                            cap(v + m + 2, m + 2)
                        if not over(s + 1) and m - 1 in XT_TURNS:
                            low_xt(dve, s + 1, XT_TURNS.index(m - 1))
                if not first(s):
                    dve.wait_ge(exps_made, s)
                    wait(dve, table_out, (s - 1) * 16)
                    router.keep_stats(dve, E, mv2, rstd2)
                    router.weigh(dve, E).then_inc(table_made, 1)
                if not over(s + 1):
                    for m in range(2):
                        take_past((s + 1) * MC + m, m, nb)
            each(dve, body)

        @block.scalar
        def _(act):
            def high_xt(s, k):
                act.wait_ge(turned, s * KD + k + 1)
                act.activation(xt_hi[:, k, :], turn_ps[:, :], ACT.Copy).then_inc(xt_hi_made, 1)

            def copy_x2t(s, k):
                act.wait_ge(turned2, (s - 1) * KD + k + 1)
                act.activation(x2t[:, k, :], turn_ps[:, :], ACT.Copy).then_inc(x2t_made, 1)

            def silu_xc(c, m):
                act.wait_ge(conv_made, c + 1)
                act.activation(gated[:, m, :], temp[m % 2][:, :], ACT.Silu)
                if m < 2:
                    wait(act, out_done, c - 1)
                else:
                    act.wait_ge(xp_done, c - 1)
                act.activation(half_hi[m % 2][:, :], temp[m % 2][:, :], ACT.Silu)\
                   .then_inc(xc_hi_made, 1)

            def high_y(v, m):
                act.wait_ge(y_made, v + 1)
                if m >= 2:
                    act.wait_ge(out_done, v - 1)
                act.activation(half_hi[m % 2][:, :], gated[:, m, :], ACT.Copy).then_inc(y_hi_made, 1)

            for k in range(KD):
                high_xt(0, k)

            def body(s, i, b):
                for m in range(MC):
                    c = s * MC + m
                    if not first(s) and m >= 5:
                        copy_x2t(s, m - 5)
                    if not over(s):
                        act.wait_ge(xs_done, c + 1)
                        wait(act, conv_made, c - 1)
                        act.activation(xs[m % 2][:, PAST:PAST + GW], chunk_ps[m % 2][:, :], ACT.Copy)
                        act.wait_ge(past_in, c + 1)
                        act.activation(past[b][:, m, :], chunk_ps[m % 2][:, GW - PAST:GW], ACT.Copy)
                        if m < 2:
                            wait(act, y_made, c - 1)
                        else:
                            act.wait_ge(xc_hi_made, c - 1)
                        act.activation(temp[m % 2][:, :], chunk_ps[m % 2][:, :], ACT.Identity,
                                       bias=conv_bias[:, m:m + 1], scale=taps[:, m, PAST:PAST + 1])\
                           .then_inc(xs_read, 1)
                        if m >= 1:
                            silu_xc(c - 1, m - 1)
                if not first(s):
                    copy_x2t(s, KD - 1)
                if not over(s):
                    silu_xc(s * MC + MC - 1, MC - 1)
                    for m in range(MC):
                        c = s * MC + m
                        act.wait_ge(z_done, c + 1)
                        wait(act, gate_made, c - 1)
                        act.activation(silu_z[m % 2][:, :], chunk_ps[m % 2][:, :], ACT.Silu)\
                           .then_inc(z_read, 1)
                        if m == 4:
                            act.wait_ge(xp_done, (s + 1) * MC)
                            act.activation(dt_parts[:, :], dt_ps[:, :], ACT.Copy)\
                               .then_inc(dt_hi_made, 1)
                def exps():
                    act.wait_ge(chosen_made, s)
                    act.activation(router.flat(router.expd), router.flat(router.shifted), ACT.Exp)\
                       .then_inc(exps_made, 1)

                if over(s):
                    exps()
                    return
                act.preload_act_table_set("natural_log_exp_and_others")
                for m in range(MC):
                    v = s * MC + m
                    if m >= 2:
                        high_y(v - 2, m - 2)
                        if not over(s + 1) and m - 2 in XT_TURNS:
                            high_xt(s + 1, XT_TURNS.index(m - 2))
                    act.wait_ge(v_capped, v + 1)
                    act.activation(chain[m % 4][:, :], chain[m % 4][:, :], ACT.Exp).then_inc(exp_done, 1)
                    act.wait_ge(exp_done, v + 1)
                    act.activation(chain[m % 4][:, :], chain[m % 4][:, :], ACT.Ln, bias=1.0)\
                       .then_inc(log_done, 1)
                    if m == 3 and not first(s):
                        exps()
                high_y(s * MC + MC - 2, MC - 2)
                high_y(s * MC + MC - 1, MC - 1)
            each(act, body)

        @block.gpsimd
        def _(pool):
            pool.wait_ge(var_made, 1)
            rstd_of(pool, mv, minus_half, rstd).then_inc(rstd_made, 1)
            pool.wait_ge(xn_made, 1)
            pool.tensor_tensor(X[0][:, :, :], X[0][:, :, :], XN[:, :, :], ALU.add).then_inc(res_made, 1)

            def store_table(s, pi, pb):
                pool.wait_ge(table_made, s)
                pool.dma_start(group(tab2, pb, pi), router.table[:, :, :]).then_inc(table_out, 16)

            def body(s, i, b):
                if not first(s):
                    pool.wait_ge(var2_made, s)
                    rstd_of(pool, mv2, minus_half, rstd2).then_inc(rstd2_made, 1)
                    pi, pb = before(i, b)
                    pool.dma_start(group(x2, pb, pi), X[pb][:, :, :]).then_inc(x2_out[pb], 16)
                    pool.dma_start(group(out_rows, pb, pi), X[pb][:, :, :]).then_inc(x2_out[pb], 16)
                if over(s):
                    store_table(s, pi, pb)
                    return
                for m in range(MC):
                    pool.wait_ge(xc_hi_made, s * MC + m + 1)
                    pool.tensor_tensor(half_lo[m % 2][:, :], gated[:, m, :], half_hi[m % 2][:, :],
                                       ALU.subtract).then_inc(xc_made, 1)
                for m in range(MC):
                    c = s * MC + m
                    pool.wait_ge(z_read, c + 1)
                    pool.wait_ge(xc_made, c + 1)
                    pool.tensor_tensor(gated[:, m, :], gated[:, m, :], silu_z[m % 2][:, :], ALU.mult)\
                        .then_inc(gate_made, 1)
                    if m == 4 and not over(s + 1):
                        pool.wait_ge(var_made, s + 2)
                        rstd_of(pool, mv, minus_half, rstd).then_inc(rstd_made, 1)
                for m in range(MC):
                    v = s * MC + m
                    pool.wait_ge(y_hi_made, v + 1)
                    pool.tensor_tensor(half_lo[m % 2][:, :], gated[:, m, :], half_hi[m % 2][:, :],
                                       ALU.subtract).then_inc(y_parts_made, 1)
                    if not over(s + 1) and m < GT:
                        if m == 0:
                            pool.wait_ge(xn_made, s + 2)
                        n = 1 - b
                        part = pool.tensor_tensor(X[n][:, m, :], X[n][:, m, :], XN[:, m, :], ALU.add)
                        if m == GT - 1:
                            part.then_inc(res_made, 1)
                if not first(s):
                    store_table(s, pi, pb)
            each(pool, body)

        @block.tensor
        def _(pe):
            def three(bank, a, b, start, stop):
                pe.matmul(bank, a[0], b[0], start=start, stop=False)
                pe.matmul(bank, a[0], b[1], start=False, stop=False)
                return pe.matmul(bank, a[1], b[0], start=False, stop=stop)

            def turn(src, k):
                for j in range(GT):
                    mm = pe.transpose(turn_ps[:, j * P:(j + 1) * P], src[:, j, k * P:(k + 1) * P],
                                      ident[:, :])
                return mm

            def turn_xt(s, k):
                if k == 0:
                    pe.wait_ge(xn_made, s + 1)
                    wait(pe, chosen_read, s - 1)
                else:
                    pe.wait_ge(xt_made, s * KD + k)
                turn(XN, k).then_inc(turned, 1)

            def in_proj(m):
                for k in range(KD):
                    cols = slice(m * P, (m + 1) * P)
                    mm = three(chunk_ps[m % 2][:, :], (w_in_hi[:, k, cols], w_in_lo[:, k, cols]),
                               (xt_hi[:, k, :], xt_lo[:, k, :]), k == 0, k == KD - 1)
                return mm

            def x_proj(s, m):
                wx, hi, lo = (w_x_hi[:, m, :], w_x_lo[:, m, :]), half_hi[m % 2], half_lo[m % 2]
                pe.wait_ge(xc_hi_made, s * MC + m + 1)
                pe.matmul(dt_ps[:, :], wx[0], hi[:, :], start=m == 0, stop=False)
                pe.matmul(dt_ps[:, :], wx[1], hi[:, :], start=False, stop=False)
                pe.wait_ge(xc_made, s * MC + m + 1)
                pe.matmul(dt_ps[:, :], wx[0], lo[:, :], start=False, stop=m == MC - 1)\
                    .then_inc(xp_done, 1)

            def out_proj(s, m):
                pe.wait_ge(y_hi_made, s * MC + m + 1)
                if m == 0:
                    wait(pe, x2_made, s)
                for j in range(GT):
                    hi = half_hi[m % 2][:, j * P:(j + 1) * P]
                    pe.matmul(out_ps[j][:, :], hi, w_out_hi[:, m, :], start=m == 0, stop=False)
                    pe.matmul(out_ps[j][:, :], hi, w_out_lo[:, m, :], start=False, stop=False)
                pe.wait_ge(y_parts_made, s * MC + m + 1)
                for j in range(GT):
                    mm = pe.matmul(out_ps[j][:, :], half_lo[m % 2][:, j * P:(j + 1) * P],
                                   w_out_hi[:, m, :], start=False, stop=m == MC - 1)
                mm.then_inc(out_done, 1)

            def dt_proj(s, m):
                v = s * MC + m
                if m == 0:
                    pe.wait_ge(dt_made, s + 1)
                elif m < 3:
                    pe.wait_ge(z_read, s * MC + MC - 2 + m)
                else:
                    pe.wait_ge(v_read, v - 2)
                pe.matmul(v_ps[m % 3][:, :], w_dt_parts[:, m * P:(m + 1) * P], dt_parts[:, :],
                          start=True, stop=True).then_inc(v_done, 1)

            for k in range(KD):
                turn_xt(0, k)

            def body(s, i, b):
                pb = before(i, b)[1]
                for m in range(MC):
                    if not over(s):
                        c = s * MC + m
                        if m == 0:
                            pe.wait_ge(xt_made, (s + 1) * KD)
                            wait(pe, v_read, s * MC)
                        elif m >= 2:
                            pe.wait_ge(xs_read, c - 1)
                        in_proj(m).then_inc(xs_done, 1)
                        if m >= 3:
                            x_proj(s, m - 3)
                    if not first(s) and m >= MC - KD:
                        k = m - (MC - KD)
                        if k == 0:
                            pe.wait_ge(xn2_made, s)
                            if over(s):
                                pe.wait_ge(xt_made, s * KD)
                        else:
                            pe.wait_ge(x2t_made, (s - 1) * KD + k)
                        turn(XN, k).then_inc(turned2, 1)
                for m in range(MC):
                    if not over(s):
                        c = s * MC + m
                        if m < 2:
                            pe.wait_ge(xs_read, c + MC - 1)
                        else:
                            pe.wait_ge(z_read, c - 1)
                        in_proj(MC + m).then_inc(z_done, 1)
                        if m < 3:
                            x_proj(s, MC - 3 + m)
                        if m == MC - 2:
                            dt_proj(s, 0)
                    if not first(s) and m == 0:
                        pe.wait_ge(x2t_made, s * KD)
                        logits(pe, turn_ps, x2t, gate_sb, KD, E).then_inc(logits_done, 1)
                    if not first(s) and m == 5:
                        pe.wait_ge(chosen_made, s)
                        turn_mask(pe, turn_ps, router, win_bits, pb).then_inc(chosen_turned, 1)
                if over(s):
                    return
                dt_proj(s, 1)
                dt_proj(s, 2)
                for m in range(MC):
                    if not over(s + 1) and m in XT_TURNS:
                        turn_xt(s + 1, XT_TURNS.index(m))
                    if m + 3 < MC:
                        dt_proj(s, m + 3)
                    out_proj(s, m)
            each(pe, body)


def kernel(**inputs):
    import numpy as np
    import concourse.bacc as bacc
    from concourse import mybir as m
    from concourse.bass_utils import run_bass_kernel_spmd

    a = {name.removeprefix("L0_"): np.asarray(value) for name, value in inputs.items()}

    def rows_on_partitions(w):
        return np.ascontiguousarray(w.reshape(-1, P, w.shape[1]).transpose(1, 0, 2))

    E, inner, D = a["ffn_w_gate"].shape
    R = a["attn_W_dt"].shape[1]
    gate_up = np.stack([a["ffn_w_gate"], a["ffn_w_up"]], 1)
    gate_up = gate_up.reshape(E, 2, inner, D // P, P).transpose(0, 4, 1, 3, 2).reshape(E, P, -1)
    down = a["ffn_w_down"].reshape(E, D, inner // P, P).transpose(0, 3, 2, 1).reshape(E, P, -1)
    arrays = {
        "x": a["attn_x"],
        "moe_w": np.ascontiguousarray(np.concatenate([gate_up, down], 2)),
        "gate_t": rows_on_partitions(a["ffn_gate_w"].T),
        "w_in": rows_on_partitions(a["attn_W_in"].T),
        "w_out": rows_on_partitions(a["attn_W_out"].T),
        "w_x": rows_on_partitions(a["attn_W_x"][:R].T),
        "w_dt": np.ascontiguousarray(a["attn_W_dt"].T),
        "conv_w": rows_on_partitions(a["attn_conv_w"][:, 0, :]),
        "conv_b": np.ascontiguousarray(a["attn_conv_b"].reshape(-1, P).T),
        "b_dt": np.ascontiguousarray(a["attn_b_dt"].reshape(-1, P).T),
    }
    nc = bacc.Bacc("TRN2", target_bir_lowering=False, num_devices=1)
    aps = {name: nc.dram_tensor(name, v.shape, m.dt.from_np(v.dtype), kind="ExternalInput").ap()
           for name, v in arrays.items()}
    shape = arrays["x"].shape
    out = nc.dram_tensor("out", shape, m.dt.float32, kind="ExternalOutput").ap()
    build_program(nc, out=out, **aps)
    result = run_bass_kernel_spmd(nc, [arrays], core_ids=[0])
    return result.results[0]["out"]
```

```python
from contextlib import ExitStack

import concourse.bass as bass
from concourse import mybir

F32 = mybir.dt.float32
F32R = mybir.dt.float32r
BF16 = mybir.dt.bfloat16
I32 = mybir.dt.int32
ALU = mybir.AluOpType
ACT = mybir.ActivationFunctionType
AX = mybir.AxisListType

P = 128
GT = 4
GW = GT * P
TOP_K = 8
CAP = 128
EPS = 1e-5
NEG = -3.0e38
CONSTANTS = 4 + 8
WIN = 8
SOFTMAX_FLOOR = -87.33654
SOFTPLUS_CAP = 40.0


def wait(eng, sem, value):
    if not isinstance(value, int) or value > 0:
        eng.wait_ge(sem, value)


def run_passes(eng, n, body):
    body(0)
    if n > 2:
        with eng.Fori(1, n - 1) as i:
            body(i)
    if n > 1:
        body(n - 1)


def known(step):
    return isinstance(step, int)


def row_stats(dve, src, stats, mv):
    for j in range(GT):
        dve.bn_stats(stats[:, j, :], src[:, j, :])
    dve.drain()
    for j in range(GT):
        dve.bn_aggr(mv[:, j, 0:2], stats[:, j, :])
    dve.drain()
    return dve.tensor_scalar(mv[:, :, 2], mv[:, :, 1], EPS, None, ALU.add)


def rstd_of(pool, mv, minus_half, rstd):
    return pool.tensor_tensor(rstd[:, :], mv[:, :, 2], minus_half[:, :], ALU.pow)


def normalise(dve, src, xn, mv, rstd):
    for j in range(GT):
        last = dve.tensor_scalar(xn[:, j, :], src[:, j, :], mv[:, j, 0:1], rstd[:, j:j + 1],
                                 ALU.subtract, ALU.mult)
    return last


class Router:

    def __init__(self, sb, tag, E):
        self.logits = sb(tag + "logits", [P, GT, E], F32)
        self.top8 = sb(tag + "top8", [P, GT, TOP_K], F32)
        self.rest = sb(tag + "rest", [P, GT, E], F32)
        self.shifted = sb(tag + "shifted", [P, GT, E], F32)
        self.expd = sb(tag + "expd", [P, GT, E], F32)
        self.chosen = sb(tag + "chosen", [P, GT, E], BF16)
        self.total = sb(tag + "total", [P, GT], F32)
        self.table = sb(tag + "table", [P, GT, E + 2], F32)

    @staticmethod
    def flat(t):
        return t[:, :, :].rearrange("p j e -> p (j e)")

    def pick(self, dve, E):
        dve.tensor_reduce(self.total[:, :], self.logits[:, :, :], AX.X, ALU.max)
        dve.drain()
        for j in range(GT):
            dve.tensor_scalar(self.shifted[:, j, :], self.logits[:, j, :], self.total[:, j:j + 1],
                              SOFTMAX_FLOOR, ALU.subtract, ALU.max)
        dve.drain()
        for j in range(GT):
            dve.max(self.top8[:, j, :], self.shifted[:, j, :])
        dve.drain()
        for j in range(GT):
            dve.match_replace(self.rest[:, j, :], self.top8[:, j, :], self.shifted[:, j, :], NEG)
        dve.drain()
        return dve.tensor_tensor(self.chosen[:, :, :], self.shifted[:, :, :], self.rest[:, :, :],
                                 ALU.not_equal)

    def keep_stats(self, dve, E, mv, rstd):
        dve.tensor_copy(self.table[:, :, E], mv[:, :, 0])
        dve.tensor_copy(self.table[:, :, E + 1], rstd[:, :])

    def weigh(self, dve, E):
        dve.tensor_tensor(self.expd[:, :, :], self.expd[:, :, :], self.chosen[:, :, :], ALU.mult)
        dve.drain()
        dve.tensor_reduce(self.total[:, :], self.expd[:, :, :], AX.X, ALU.add)
        dve.drain()
        dve.reciprocal(self.total[:, :], self.total[:, :])
        dve.drain()
        return dve.scalar_tensor_tensor(
            out=self.table[:, :, 0:E], in0=self.expd[:, :, :], scalar=0.5,
            in1=self.total[:, :].rearrange("p (j a) -> p j a", a=1).broadcast_to([P, GT, E]),
            op0=ALU.mult, op1=ALU.mult)


def build_program(nc, x, moe_w, gate_t, w_in, w_out, w_x, w_dt, conv_w, conv_b, b_dt, out):
    B, L, D = x.shape
    T = B * L
    E = gate_t.shape[2]
    KD = D // P
    MC = w_out.shape[1]
    DI = MC * P
    R = w_dt.shape[0]
    IN = (moe_w.shape[2] // (2 * KD + D // P)) if D == 512 else 0
    KI = IN // P
    NG = L // GW
    STEPS = B * NG
    TAPS = conv_w.shape[2]
    PAST = TAPS - 1
    assert B == 2 and E == 64 and 4 * R == P and GT * E <= 512 and D == 512
    assert moe_w.shape[2] == 2 * KD * IN + KI * D

    x_rows = x.rearrange("b l d -> (b l) d")
    out_rows = out.rearrange("b l d -> (b l) d")
    x1 = nc.dram_tensor("x1", [T, D], F32, kind="Internal").ap()
    x2 = nc.dram_tensor("x2", [T, D], F32, kind="Internal").ap()
    tab1 = nc.dram_tensor("tab1", [T, E + 2], F32, kind="Internal").ap()
    tab2 = nc.dram_tensor("tab2", [T, E + 2], F32, kind="Internal").ap()

    def group(rows, b, i):
        g = rows.rearrange("(b g j p) n -> b g p j n", b=B, j=GT, p=P)
        if known(i):
            return g[b, i]
        return g[b, bass.ds(i, 1)].rearrange("g p j n -> p (g j) n")

    with ExitStack() as top:
        def top_sb(name, shape, dt):
            return top.enter_context(nc.sbuf_tensor(name, shape, dt))

        ident = top_sb("ident", [P, P], F32)
        minus_half = top_sb("minus_half", [P, GT], F32)
        win_bits = top_sb("win_bits", [P, P // WIN], BF16)
        gate_sb = top_sb("gate_sb", [P, KD, E], F32)
        windows = top_sb("windows", [P, L // WIN], F32)
        slot_token = top_sb("slot_token", [P, E], I32)

        first_routing(nc, gate_t, x_rows, x1, tab1, group, NG, KD, E, D, ident, win_bits, minus_half, gate_sb, windows)
        with MixerWeights(nc, w_in, w_x, w_dt, KD, MC, R) as mixer_w:
            with WeightRing(nc, moe_w, KD * IN, KI * D, "a") as ring:
                find_slots(nc, T, L, E, ident, windows, slot_token, ring, mixer_w, "a")
                experts(nc, x_rows, tab1, x1, ring, T, E, D, KD, IN, KI, ident, slot_token, "a")
            mixer(nc, x1, x2, out_rows, tab2, group, NG, KD, MC, R, PAST, E, D, L, mixer_w, w_out,
                  conv_w, conv_b, b_dt, ident, win_bits, minus_half, gate_sb, windows)
        with WeightRing(nc, moe_w, KD * IN, KI * D, "b") as ring:
            find_slots(nc, T, L, E, ident, windows, slot_token, ring, None, "b")
            experts(nc, x2, tab2, out_rows, ring, T, E, D, KD, IN, KI, ident, slot_token, "b")


def make_constants(pool, made, ident, win_bits, minus_half):
    pool.memset(minus_half[:, :], -0.5).then_inc(made, 1)
    pool.memset(ident[:, :], 0.0).then_inc(made, 1)
    pool.memset(win_bits[:, :], 0.0).then_inc(made, 1)
    pool.wait_ge(made, 3)
    pool.affine_select(out=ident[:, :], in_=ident[:, :], compare_op=ALU.not_equal, fill=1.0,
                       base=0, pattern=[[-1, P]], channel_multiplier=1).then_inc(made, 1)
    for t in range(WIN):
        pool.wait_ge(made, 4 + t)
        pool.affine_select(out=win_bits[:, :], in_=win_bits[:, :], compare_op=ALU.not_equal,
                           fill=float(2 ** (WIN - 1 - t)), base=-t,
                           pattern=[[-WIN, P // WIN]], channel_multiplier=1).then_inc(made, 1)
    pool.wait_ge(made, CONSTANTS)


def first_routing(nc, gate_t, x_rows, x1, tab1, group, NG, KD, E, D, ident, win_bits, minus_half, gate_sb, windows):
    STEPS = 2 * NG
    with ExitStack() as ctx:
        def sb(name, shape, dt):
            return ctx.enter_context(nc.sbuf_tensor("r_" + name, shape, dt))

        def psum(name):
            return ctx.enter_context(nc.psum_tensor("r_" + name, [P, 512], F32))

        def sem(name):
            return ctx.enter_context(nc.semaphore("r_" + name))

        X = [sb(f"x{b}", [P, GT, D], F32) for b in range(2)]
        XN = [sb(f"xn{b}", [P, GT, D], F32) for b in range(2)]
        XT = [sb(f"xt{b}", [P, KD, GW], F32) for b in range(2)]
        stats = sb("stats", [P, GT, 6], F32)
        mv = [sb(f"mv{b}", [P, GT, 3], F32) for b in range(2)]
        neg_mean = [sb(f"neg_mean{b}", [P, GT], F32) for b in range(2)]
        rstd = [sb(f"rstd{b}", [P, GT], F32) for b in range(2)]
        shift = [sb(f"shift{b}", [P, GT], F32) for b in range(2)]
        rt = [Router(sb, f"rt{b}_", E) for b in range(2)]
        turn_ps = [psum(f"turn{n}") for n in range(2)]
        logit_ps = [psum(f"logit{b}") for b in range(2)]
        chosen_ps = [psum(f"chosen{b}") for b in range(2)]

        x_in = [sem(f"x_in{b}") for b in range(2)]
        x1_out = [sem(f"x1_out{b}") for b in range(2)]
        constants_made = sem("constants_made")
        gate_loaded = sem("gate_loaded")
        var_made = sem("var_made")
        rstd_made = sem("rstd_made")
        shift_made = sem("shift_made")
        xn_made = sem("xn_made")
        turned = sem("turned")
        xt_made = sem("xt_made")
        logits_done = sem("logits_done")
        logits_read = sem("logits_read")
        chosen_made = sem("chosen_made")
        exp_made = sem("exp_made")
        chosen_turned = sem("chosen_turned")
        table_made = sem("table_made")
        table_out = [sem(f"table_out{b}") for b in range(2)]
        block = ctx.enter_context(nc.Block())

        def each(eng, body):
            def one_pass(i):
                for b in range(2):
                    body(i * 2 + b, i, b)
            run_passes(eng, NG, one_pass)
            one_pass(NG)

        def early(s):
            return known(s) and s < 2

        def over(s):
            return known(s) and s >= STEPS

        @block.sync
        def _(sp):
            for b in range(2):
                sp.dma_start(X[b][:, :, :], group(x_rows, b, 0)).then_inc(x_in[b], 16)
            sp.dma_start(gate_sb[:, :, :], gate_t).then_inc(gate_loaded, 16)

            def one_pass(i):
                for b in range(2):
                    sp.wait_ge(x_in[b], i * 16 + 16)
                    sp.dma_start(group(x1, b, i), X[b][:, :, :]).then_inc(x1_out[b], 16)
                if known(i) and i == NG - 1:
                    return
                for b in range(2):
                    sp.wait_ge(xn_made, (i * 2 + b + 1) * GT)
                    sp.wait_ge(x1_out[b], i * 16 + 16)
                    sp.dma_start(X[b][:, :, :], group(x_rows, b, i + 1)).then_inc(x_in[b], 16)
            run_passes(sp, NG, one_pass)
            for b in range(2):
                sp.wait_ge(x1_out[b], 16 * NG)

        @block.vector
        def _(dve):
            def body(s, i, b):
                r = rt[b]
                if not early(s):
                    dve.wait_ge(logits_done, s - 1)
                    dve.tensor_copy(r.flat(r.logits), logit_ps[b][:, 0:GT * E])\
                       .then_inc(logits_read, 1)
                    dve.drain()
                    wait(dve, table_out[b], (i - 1) * 16)
                    r.keep_stats(dve, E, mv[b], rstd[b])
                    r.pick(dve, E).then_inc(chosen_made, 1)
                if not over(s):
                    dve.wait_ge(x_in[b], i * 16 + 16)
                    row_stats(dve, X[b], stats, mv[b])
                    dve.tensor_scalar(neg_mean[b][:, :], mv[b][:, :, 0], -1.0, None, ALU.mult)\
                       .then_inc(var_made, 1)
                    dve.drain()
                if not early(s):
                    dve.wait_ge(exp_made, s - 1)
                    r.weigh(dve, E).then_inc(table_made, 1)
                    dve.wait_ge(chosen_turned, s - 1)
                    h = slice(64 * b, 64 * b + 64)
                    dve.tensor_copy(windows[h, bass.ds((i - 1) * (GW // WIN), GW // WIN)],
                                    chosen_ps[b][h, 0:GW // WIN])
            each(dve, body)

        @block.scalar
        def _(act):
            def body(s, i, b):
                if not early(s):
                    act.wait_ge(chosen_made, s - 1)
                    act.activation(rt[b].flat(rt[b].expd), rt[b].flat(rt[b].shifted), ACT.Exp)\
                       .then_inc(exp_made, 1)
                if over(s):
                    return
                act.wait_ge(shift_made, s + 1)
                for j in range(GT + 1):
                    if j < GT:
                        act.activation(XN[b][:, j, :], X[b][:, j, :], ACT.Identity,
                                       bias=shift[b][:, j:j + 1], scale=rstd[b][:, j:j + 1])\
                           .then_inc(xn_made, 1)
                    if j >= 1:
                        t = j - 1
                        act.wait_ge(turned, s * GT + t + 1)
                        act.activation(XT[b][:, :, t * P:(t + 1) * P],
                                       turn_ps[t % 2][:, :].rearrange("p (k t) -> p k t", k=KD),
                                       ACT.Copy).then_inc(xt_made, 1)
            each(act, body)

        @block.tensor
        def _(pe):
            pe.wait_ge(constants_made, CONSTANTS)
            pe.wait_ge(gate_loaded, 16)

            def body(s, i, b):
                if not early(s):
                    pe.wait_ge(chosen_made, s - 1)
                    turn_mask(pe, chosen_ps[b], rt[b], win_bits, b).then_inc(chosen_turned, 1)
                if over(s):
                    return
                for j in range(GT + 1):
                    if j < GT:
                        pe.wait_ge(xn_made, s * GT + j + 1)
                        wait(pe, xt_made, s * GT + j - 1)
                        for k in range(KD):
                            mm = pe.transpose(turn_ps[j % 2][:, k * P:(k + 1) * P],
                                              XN[b][:, j, k * P:(k + 1) * P], ident[:, :])
                        mm.then_inc(turned, 1)
                    if j == 1 and not early(s):
                        pe.wait_ge(logits_read, s - 1)
                    if j >= 1:
                        pe.wait_ge(xt_made, s * GT + j)
                        mm = tile_logits(pe, logit_ps[b], XT[b], gate_sb, KD, E, j - 1)
                mm.then_inc(logits_done, 1)
            each(pe, body)

        @block.gpsimd
        def _(pool):
            make_constants(pool, constants_made, ident, win_bits, minus_half)

            def body(s, i, b):
                if not over(s):
                    pool.wait_ge(var_made, s + 1)
                    rstd_of(pool, mv[b], minus_half, rstd[b]).then_inc(rstd_made, 1)
                    pool.wait_ge(rstd_made, s + 1)
                    pool.tensor_tensor(shift[b][:, :], neg_mean[b][:, :], rstd[b][:, :], ALU.mult)\
                        .then_inc(shift_made, 1)
                if not early(s):
                    pool.wait_ge(table_made, s - 1)
                    pool.dma_start(group(tab1, b, i - 1), rt[b].table[:, :, :])\
                        .then_inc(table_out[b], 16)
            each(pool, body)
            for b in range(2):
                pool.wait_ge(table_out[b], 16 * NG)


def logits(pe, bank, xt, gate_sb, KD, E):
    for j in range(GT):
        mm = tile_logits(pe, bank, xt, gate_sb, KD, E, j)
    return mm


def tile_logits(pe, bank, xt, gate_sb, KD, E, j):
    for k in range(KD):
        mm = pe.matmul(bank[:, j * E:(j + 1) * E], xt[:, k, j * P:(j + 1) * P], gate_sb[:, k, :],
                       start=(k == 0), stop=(k == KD - 1))
    return mm


def turn_mask(pe, bank, router, win_bits, b):
    n = P // WIN
    for j in range(GT):
        mm = pe.matmul(bank[64 * b:64 * b + 64, j * n:(j + 1) * n], router.chosen[:, j, :],
                       win_bits[:, :], start=True, stop=True)
    return mm


RING = 4


class WeightRing(ExitStack):

    def __init__(self, nc, moe_w, GU, DN, tag):
        super().__init__()
        self.moe_w = moe_w
        self.parts = ((0, GU), (GU, GU), (2 * GU, DN))
        self.W = [self.enter_context(nc.sbuf_tensor(f"m{tag}_w{k}", [P, 2 * GU + DN], F32))
                  for k in range(RING)]
        self.landed = [[self.enter_context(nc.semaphore(f"m{tag}_{name}_in{k}")) for k in range(RING)]
                       for name in ("gate", "up", "down")]

    def load(self, sp, e, k, part):
        at, n = self.parts[part]
        rows = self.moe_w[e] if known(e) else \
            self.moe_w[bass.ds(e, 1)].rearrange("a p n -> p (a n)")
        sp.dma_start(self.W[k][:, at:at + n], rows[:, at:at + n]).then_inc(self.landed[part][k], 16)


class MixerWeights(ExitStack):

    def __init__(self, nc, w_in, w_x, w_dt, KD, MC, R):
        super().__init__()
        DI = MC * P

        def sb(name, shape):
            return self.enter_context(nc.sbuf_tensor("w_" + name, shape, F32R))

        self.nc, self.w_dt, self.R, self.DI = nc, w_dt, R, DI
        self.in_hi, self.in_lo = sb("in_hi", [P, KD, 2 * DI]), sb("in_lo", [P, KD, 2 * DI])
        self.x_hi, self.x_lo = sb("x_hi", [P, MC, P]), sb("x_lo", [P, MC, P])
        self.dt_parts = sb("dt_parts", [P, DI])
        four = "p m (c r) -> p m c r"
        self.pieces = [(2 * DI, w_in[:, k, :], lambda stage: stage,
                        self.in_hi[:, k, :], self.in_lo[:, k, :]) for k in range(KD)]
        self.pieces += [(MC * R, w_x.rearrange("p m r -> p (m r)"),
                         lambda stage: stage[:, 0:MC * R].rearrange("p (m a r) -> p m a r", m=MC, a=1)
                         .broadcast_to([P, MC, 4, R]),
                         self.x_hi[:, :, :].rearrange(four, c=4),
                         self.x_lo[:, :, :].rearrange(four, c=4))]

    def begin(self, ctx):
        nc = self.nc
        self.stage = [ctx.enter_context(nc.sbuf_tensor(f"w_stage{k}", [P, 2 * self.DI], F32))[:, :]
                      for k in range(2)]
        self.landed = [ctx.enter_context(nc.semaphore(f"w_landed{k}")) for k in range(2)]
        self.hi_made = ctx.enter_context(nc.semaphore("w_hi_made"))
        self.lo_made = ctx.enter_context(nc.semaphore("w_lo_made"))
        self.last = len(self.pieces)
        self.dt_landed = 16 * (self.last // 2 + 4)

    def load(self, sp):
        for n, (cols, src, _, _, _) in enumerate(self.pieces):
            wait(sp, self.lo_made, n - 1)
            sp.dma_start(self.stage[n % 2][:, 0:cols], src).then_inc(self.landed[n % 2], 16)
        n = self.last
        sp.wait_ge(self.lo_made, n - 1)
        for c in range(4):
            sp.dma_start(self.stage[n % 2][c * self.R:(c + 1) * self.R, 0:self.DI], self.w_dt)\
              .then_inc(self.landed[n % 2], 16)

    def make_hi(self, act):
        for n, (_, _, view, hi, _) in enumerate(self.pieces):
            act.wait_ge(self.landed[n % 2], 16 * (n // 2 + 1))
            act.activation(hi, view(self.stage[n % 2]), ACT.Copy).then_inc(self.hi_made, 1)
        n = self.last
        act.wait_ge(self.landed[n % 2], self.dt_landed)
        act.activation(self.dt_parts[:, :], self.stage[n % 2][:, 0:self.DI], ACT.Copy)\
           .then_inc(self.hi_made, 1)

    def make_lo(self, pool):
        for n, (_, _, view, hi, lo) in enumerate(self.pieces):
            pool.wait_ge(self.hi_made, n + 1)
            pool.tensor_tensor(lo, view(self.stage[n % 2]), hi, ALU.subtract).then_inc(self.lo_made, 1)
        pool.wait_ge(self.hi_made, self.last + 1)
        pool.wait_ge(self.lo_made, self.last)
        rows = slice(2 * self.R, 4 * self.R)
        pool.tensor_tensor(self.dt_parts[rows, :], self.stage[self.last % 2][rows, 0:self.DI],
                           self.dt_parts[rows, :], ALU.subtract).then_inc(self.lo_made, 1)


def find_slots(nc, T, L, E, ident, windows, slot_token, ring, mixer_w, tag):
    LW, NW = L // WIN, T // WIN
    bits = 2 ** WIN
    flag = 2 * bits * NW
    assert LW >= 2 * CAP and 2 * flag <= 2 ** 24 and NW & (NW - 1) == 0
    with ExitStack() as ctx:
        def sb(name, shape, dt):
            return ctx.enter_context(nc.sbuf_tensor(f"f{tag}_{name}", shape, dt))

        def sem(name):
            return ctx.enter_context(nc.semaphore(f"f{tag}_{name}"))

        number = sb("number", [P, LW], I32)
        back = sb("back", [P, WIN], I32)
        flags = sb("flags", [P, LW], F32)
        win_keys = sb("win_keys", [P, LW], F32)
        best_win = sb("best_win", [P, CAP], F32)
        packed = sb("packed", [P, CAP], I32)
        first = sb("first", [P, CAP], I32)
        bit = sb("bit", [P, CAP, WIN], I32)
        keys = sb("keys", [P, CAP, WIN], F32)
        best = sb("best", [P, CAP], F32)
        both = sb("both", [E, 2 * CAP], F32)
        final = sb("final", [E, CAP], F32)
        raised = sb("raised", [P, E], F32)
        turned_ps = ctx.enter_context(nc.psum_tensor(f"f{tag}_turned", [P, E], F32))
        numbered = sem("numbered")
        final_made = sem("final_made")
        final_turned = sem("final_turned")
        if mixer_w:
            mixer_w.begin(ctx)
        block = ctx.enter_context(nc.Block())

        if mixer_w:
            @block.scalar
            def _(act):
                mixer_w.make_hi(act)

        @block.sync
        def _(sp):
            if mixer_w:
                mixer_w.load(sp)
            for k in range(RING):
                for part in range(3):
                    ring.load(sp, k, k, part)

        @block.gpsimd
        def _(pool):
            for b in range(2):
                pool.iota(number[64 * b:64 * b + 64, :], [[-bits, LW]], base=bits * (NW - b * LW),
                          channel_multiplier=0).then_inc(numbered, 1)
            pool.wait_ge(numbered, 2)
            pool.iota(back[:, :], [[-1, WIN]], base=0, channel_multiplier=0).then_inc(numbered, 1)
            if mixer_w:
                mixer_w.make_lo(pool)

        @block.vector
        def _(dve):
            def take(keys, best, n):
                for r in range(n // TOP_K):
                    eight = best[:, r * TOP_K:(r + 1) * TOP_K]
                    rest = keys[:, r * TOP_K:]
                    dve.max(eight, rest)
                    dve.drain()
                    dve.match_replace(rest, eight, rest, 0.0)
                    dve.drain()

            dve.tensor_scalar(flags[:, :], windows[:, :], 0.0, float(flag), ALU.is_gt, ALU.mult)
            dve.wait_ge(numbered, 3)
            dve.scalar_tensor_tensor(out=win_keys[:, :], in0=windows[:, :], scalar=1.0,
                                     in1=number[:, :], op0=ALU.mult, op1=ALU.add)
            dve.drain()
            dve.tensor_tensor(win_keys[:, :], win_keys[:, :], flags[:, :], ALU.add)
            dve.drain()
            take(win_keys[:, :], best_win[:, :], CAP)
            dve.tensor_copy(packed[:, :], best_win[:, :])
            dve.drain()
            shift = WIN - (WIN.bit_length() - 1)
            dve.tensor_scalar(first[:, :], packed[:, :], shift, 2 * T - WIN,
                              ALU.logical_shift_right, ALU.bitwise_and)
            for t in range(WIN):
                dve.tensor_scalar(bit[:, :, t], packed[:, :], WIN - 1 - t, 1,
                                  ALU.logical_shift_right, ALU.bitwise_and)
            dve.drain()
            for t in range(WIN):
                dve.scalar_tensor_tensor(out=keys[:, :, t], in0=bit[:, :, t], scalar=float(T),
                                         in1=first[:, :], op0=ALU.mult, op1=ALU.add)
            dve.drain()
            dve.tensor_tensor(keys[:, :, :], keys[:, :, :],
                              back[:, :].rearrange("p (a t) -> p a t", a=1)
                              .broadcast_to([P, CAP, WIN]), ALU.add)
            dve.drain()
            take(keys[:, :, :].rearrange("p c t -> p (c t)"), best[:, :], CAP)
            for b in range(2):
                dve.tensor_copy(both[:, b * CAP:(b + 1) * CAP], best[64 * b:64 * b + 64, :])
            dve.drain()
            take(both[:, :], final[:, :], CAP)
            dve.drain().then_inc(final_made, 1)
            dve.wait_ge(final_turned, 1)
            dve.tensor_scalar(raised[:, :], turned_ps[:, :], float(T), float(T), ALU.is_gt, ALU.mult)
            dve.drain()
            dve.tensor_tensor(raised[:, :], raised[:, :], turned_ps[:, :], ALU.subtract)
            dve.drain()
            dve.tensor_scalar(slot_token[:, :], raised[:, :], float(T), None, ALU.add)

        @block.tensor
        def _(pe):
            pe.wait_ge(final_made, 1)
            pe.transpose(turned_ps[:, :], final[:, :], ident[0:E, 0:E]).then_inc(final_turned, 1)


def experts(nc, src, table, dst, ring, T, E, D, KD, IN, KI, ident, slot_token, tag):
    GU = KD * IN
    with ExitStack() as ctx:
        def sb(name, shape, dt):
            return ctx.enter_context(nc.sbuf_tensor(f"m{tag}_{name}", shape, dt))

        def psum(name, n):
            return ctx.enter_context(nc.psum_tensor(f"m{tag}_{name}", [P, n], F32))

        def sem(name):
            return ctx.enter_context(nc.semaphore(f"m{tag}_{name}"))

        W = ring.W
        XG = [sb(f"xg{k}", [P, D], F32) for k in range(RING)]
        tab = [sb(f"tab{k}", [P, E + 2], F32) for k in range(RING)]
        fetched = [sb(f"fetched{k}", [P, 1], I32) for k in range(RING)]
        stored = [sb(f"stored{k}", [P, 1], I32) for k in range(RING)]
        zero = sb("zero", [P, 1], F32)
        mark = sb("mark", [P, 2 * RING], F32)
        XN = [sb(f"xn{k}", [P, D], F32) for k in range(2)]
        XT = [sb(f"xt{k}", [P, KD, P], F32) for k in range(2)]
        act_g = [sb(f"act_g{k}", [P, IN], F32) for k in range(2)]
        gu = [sb(f"gu{k}", [P, IN], F32) for k in range(2)]
        guT = [sb(f"guT{k}", [P, KI, P], F32) for k in range(2)]
        result = [sb(f"result{k}", [P, D], F32) for k in range(2)]
        x_ps = psum("x", D)
        gate_ps = psum("gate", IN)
        up_ps = psum("up", IN)
        gu_ps = psum("gu", IN)
        down_ps = [psum(f"down{k}", D) for k in range(2)]

        gate_in, up_in, down_in = ring.landed
        zeroed = sem("zeroed")
        held = sem("held")
        indexed = sem("indexed")
        stored_made = sem("stored_made")
        rows_in = [sem(f"rows_in{k}") for k in range(RING)]
        tab_in = [sem(f"tab_in{k}") for k in range(RING)]
        added = sem("added")
        xn_made = sem("xn_made")
        x_turned = sem("x_turned")
        xt_made = sem("xt_made")
        gate_done = sem("gate_done")
        up_done = sem("up_done")
        act_made = sem("act_made")
        gu_made = sem("gu_made")
        gu_turned = sem("gu_turned")
        guT_made = sem("guT_made")
        down_done = sem("down_done")
        result_made = sem("result_made")
        block = ctx.enter_context(nc.Block())

        def each(eng, body):
            def one_pass(i):
                for k in range(RING):
                    body(i, k, i * RING + k)
            run_passes(eng, E // RING, one_pass)

        def beyond(e):
            return known(e) and e >= E

        @block.sync
        def _(sp):
            def body(i, k, e):
                if known(i) and i == 0:
                    return
                for part, done in enumerate((gate_done, up_done, down_done)):
                    sp.wait_ge(done, e - RING + 1)
                    ring.load(sp, e, k, part)
            each(sp, body)

        @block.gpsimd
        def _(pool):
            def hold(e, k, which):
                wait(pool, held, 2 * (e - RING) + which + 1)
                at = slice(2 * k + which, 2 * k + which + 1)
                pool.tensor_tensor(mark[:, at], zero[:, :], zero[:, :], ALU.add).then_inc(held, 1)

            def fetch(e, k):
                wait(pool, xn_made, e - RING + 1)
                pool.tensor_copy(fetched[k][:, :], slot_token[:, bass.ds(e, 1)]).then_inc(indexed, 1)
                pool.wait_ge(indexed, e + 1)
                hold(e, k, 0)
                for rows, there, landed in ((XG[k], src, rows_in[k]), (tab[k], table, tab_in[k])):
                    pool.indirect_dma_start(
                        out=rows[:, :], out_offset=None, in_=there,
                        in_offset=bass.IndirectOffsetOnAxis(ap=fetched[k][:, :], axis=0))\
                        .then_inc(landed, 16)

            pool.memset(zero[:, :], 0.0).then_inc(zeroed, 1)
            pool.wait_ge(zeroed, 1)
            for e in range(RING - 1):
                fetch(e, e)

            def body(i, k, e):
                pool.tensor_copy(stored[k][:, :], slot_token[:, bass.ds(e, 1)]).then_inc(stored_made, 1)
                if not beyond(e + RING - 1):
                    fetch(e + RING - 1, (k + RING - 1) % RING)
                pool.wait_ge(stored_made, e + 1)
                wait(pool, added, e * 16)
                pool.wait_ge(result_made, e + 1)
                hold(e, k, 1)
                pool.indirect_dma_start(
                    out=dst, out_offset=bass.IndirectOffsetOnAxis(ap=stored[k][:, :], axis=0),
                    in_=result[k % 2][:, :], in_offset=None, compute_op=ALU.add).then_inc(added, 16)
            each(pool, body)
            pool.wait_ge(added, 16 * E)

        @block.vector
        def _(dve):
            def norm(i, e, k):
                dve.wait_ge(rows_in[k], i * 16 + 16)
                wait(dve, x_turned, e - 1)
                dve.wait_ge(tab_in[k], i * 16 + 16)
                dve.tensor_scalar(XN[k % 2][:, :], XG[k][:, :], tab[k][:, E:E + 1],
                                  tab[k][:, E + 1:E + 2], ALU.subtract, ALU.mult).then_inc(xn_made, 1)

            def mul(e, k):
                dve.wait_ge(act_made, e + 1)
                dve.wait_ge(up_done, e + 1)
                dve.tensor_tensor(gu[k % 2][:, :], act_g[k % 2][:, :], up_ps[:, :], ALU.mult)\
                   .then_inc(gu_made, 1)

            norm(0, 0, 0)
            norm(0, 1, 1)
            mul(0, 0)

            def body(i, k, e):
                if not beyond(e + 2):
                    norm(i + (k + 2) // RING, e + 2, (k + 2) % RING)
                if not beyond(e + 1):
                    mul(e + 1, k + 1)
                dve.wait_ge(down_done, e + 1)
                wait(dve, added, (e - 1) * 16)
                dve.tensor_scalar(result[k % 2][:, :], down_ps[k % 2][:, :],
                                  tab[k][:, bass.ds(e, 1)], None, ALU.mult).then_inc(result_made, 1)
            each(dve, body)

        @block.scalar
        def _(act):
            def copy_xt(e, k):
                act.wait_ge(x_turned, e + 1)
                act.activation(XT[k % 2][:, :, :].rearrange("p k c -> p (k c)"), x_ps[:, :], ACT.Copy)\
                   .then_inc(xt_made, 1)

            def silu(e, k):
                act.wait_ge(gate_done, e + 1)
                act.activation(act_g[k % 2][:, :], gate_ps[:, :], ACT.Silu).then_inc(act_made, 1)

            copy_xt(0, 0)
            silu(0, 0)
            copy_xt(1, 1)

            def body(i, k, e):
                if not beyond(e + 1):
                    silu(e + 1, k + 1)
                act.wait_ge(gu_turned, e + 1)
                act.activation(guT[k % 2][:, :, :].rearrange("p k c -> p (k c)"), gu_ps[:, :], ACT.Copy)\
                   .then_inc(guT_made, 1)
                if not beyond(e + 2):
                    copy_xt(e + 2, k)
            each(act, body)

        @block.tensor
        def _(pe):
            def turn_x(e, k):
                pe.wait_ge(xn_made, e + 1)
                for c in range(KD):
                    mm = pe.transpose(x_ps[:, c * P:(c + 1) * P], XN[k % 2][:, c * P:(c + 1) * P],
                                      ident[:, :])
                mm.then_inc(x_turned, 1)

            def project(bank, k, part):
                w = W[k % RING]
                for c in range(KD):
                    at = part * GU + c * IN
                    mm = pe.matmul(bank[:, :], XT[k % 2][:, c, :], w[:, at:at + IN],
                                   start=(c == 0), stop=(c == KD - 1))
                return mm

            def gate(i, e, k):
                pe.wait_ge(gate_in[k % RING], i * 16 + 16)
                pe.wait_ge(xt_made, e + 1)
                wait(pe, act_made, e)
                project(gate_ps, k, 0).then_inc(gate_done, 1)

            def up(i, e, k):
                pe.wait_ge(up_in[k % RING], i * 16 + 16)
                project(up_ps, k, 1).then_inc(up_done, 1)

            turn_x(0, 0)
            gate(0, 0, 0)
            up(0, 0, 0)
            turn_x(1, 1)

            def body(i, k, e):
                if not beyond(e + 1):
                    gate(i + (k + 1) // RING, e + 1, k + 1)
                pe.wait_ge(gu_made, e + 1)
                for c in range(KI):
                    mm = pe.transpose(gu_ps[:, c * P:(c + 1) * P], gu[k % 2][:, c * P:(c + 1) * P],
                                      ident[:, :])
                mm.then_inc(gu_turned, 1)
                if not beyond(e + 1):
                    up(i + (k + 1) // RING, e + 1, k + 1)
                if not beyond(e + 2):
                    turn_x(e + 2, k)
                pe.wait_ge(guT_made, e + 1)
                pe.wait_ge(down_in[k], i * 16 + 16)
                wait(pe, result_made, e - 1)
                for c in range(KI):
                    at = 2 * GU + c * D
                    mm = pe.matmul(down_ps[k % 2][:, :], guT[k % 2][:, c, :], W[k][:, at:at + D],
                                   start=(c == 0), stop=(c == KI - 1))
                mm.then_inc(down_done, 1)
            each(pe, body)


def mixer(nc, x1, x2, out_rows, tab2, group, NG, KD, MC, R, PAST, E, D, L, mixer_w, w_out,
          conv_w, conv_b, b_dt, ident, win_bits, minus_half, gate_sb, windows):
    STEPS = 2 * NG
    DI = MC * P
    XT_TURNS = (1, 3, 4, 5)
    assert len(XT_TURNS) == KD
    with ExitStack() as ctx:
        def sb(name, shape, dt):
            return ctx.enter_context(nc.sbuf_tensor("c_" + name, shape, dt))

        def psum(name):
            return ctx.enter_context(nc.psum_tensor("c_" + name, [P, GW], F32))

        def sem(name):
            return ctx.enter_context(nc.semaphore("c_" + name))

        w_in_hi, w_in_lo = mixer_w.in_hi, mixer_w.in_lo
        w_x_hi, w_x_lo = mixer_w.x_hi, mixer_w.x_lo
        w_dt_parts = mixer_w.dt_parts
        w_out_hi = sb("w_out_hi", [P, MC, D], F32R)
        w_out_lo = sb("w_out_lo", [P, MC, D], F32R)
        taps = sb("taps", [P, MC, PAST + 1], F32)
        conv_bias = sb("conv_bias", [P, MC], F32)
        dt_bias = sb("dt_bias", [P, MC], F32)
        X = [sb(f"x{b}", [P, GT, D], F32) for b in range(2)]
        XN = sb("xn", [P, GT, D], F32)
        xt_hi = sb("xt_hi", [P, KD, GW], F32R)
        xt_lo = sb("xt_lo", [P, KD, GW], F32R)
        x2t = sb("x2t", [P, KD, GW], F32)
        gated = sb("gated", [P, MC, GW], F32)
        half_hi = [sb(f"half_hi{k}", [P, GW], F32R) for k in range(2)]
        half_lo = [sb(f"half_lo{k}", [P, GW], F32R) for k in range(2)]
        xs = [sb(f"xs{k}", [P, PAST + GW], F32) for k in range(2)]
        temp = [sb(f"temp{k}", [P, GW], F32) for k in range(2)]
        silu_z = [sb(f"silu_z{k}", [P, GW], F32) for k in range(2)]
        chain = temp + silu_z
        dt_parts = sb("dt_parts", [P, GW], F32R)
        past = [sb(f"past{b}", [P, MC, PAST], F32) for b in range(2)]
        stats = sb("stats", [P, GT, 6], F32)
        mv, mv2 = (sb(f"mv{n}", [P, GT, 3], F32) for n in (1, 2))
        rstd, rstd2 = (sb(f"rstd{n}", [P, GT], F32) for n in (1, 2))
        router = Router(sb, "rt_", E)
        x_in = [sem(f"x_in{b}") for b in range(2)]

        with ExitStack() as prep:
            flat = "p k n -> p (k n)"
            half = MC // 2
            parts = [slice(h * half, (h + 1) * half) for h in range(2)]
            assert D == GW
            landed = [prep.enter_context(nc.semaphore(f"p_landed{h}")) for h in range(2)]
            small_in = prep.enter_context(nc.semaphore("p_small_in"))
            hi_made = prep.enter_context(nc.semaphore("p_hi_made"))
            block = prep.enter_context(nc.Block())

            @block.sync
            def _(sp):
                for h, at in enumerate(parts):
                    sp.dma_start(gated[:, at, :], w_out[:, at, :]).then_inc(landed[h], 16)
                for dst, src in ((taps, conv_w), (conv_bias, conv_b), (dt_bias, b_dt)):
                    sp.dma_start(dst[:], src).then_inc(small_in, 16)
                for b in range(2):
                    sp.dma_start(X[b][:, :, :], group(x1, b, 0)).then_inc(x_in[b], 16)
                sp.wait_ge(small_in, 48)

            @block.scalar
            def _(act):
                for h, at in enumerate(parts):
                    act.wait_ge(landed[h], 16)
                    act.activation(w_out_hi[:, at, :].rearrange(flat), gated[:, at, :].rearrange(flat),
                                   ACT.Copy).then_inc(hi_made, 1)

            @block.vector
            def _(dve):
                for b in range(2):
                    dve.memset(past[b][:, :, :], 0.0)
                for h, at in enumerate(parts):
                    dve.wait_ge(hi_made, h + 1)
                    dve.tensor_tensor(w_out_lo[:, at, :].rearrange(flat),
                                      gated[:, at, :].rearrange(flat),
                                      w_out_hi[:, at, :].rearrange(flat), ALU.subtract)

        chunk_ps = [psum(f"chunk{k}") for k in range(2)]
        dt_ps = psum("dt")
        v_ps = [dt_ps] + chunk_ps
        turn_ps = psum("turn")
        out_ps = [psum(f"out{j}") for j in range(GT)]

        var_made = sem("var_made")
        rstd_made = sem("rstd_made")
        xn_made = sem("xn_made")
        res_made = sem("res_made")
        turned = sem("turned")
        xt_hi_made = sem("xt_hi_made")
        xt_made = sem("xt_made")
        xs_done = sem("xs_done")
        xs_read = sem("xs_read")
        past_in = sem("past_in")
        conv_made = sem("conv_made")
        xc_hi_made = sem("xc_hi_made")
        xc_made = sem("xc_made")
        xp_done = sem("xp_done")
        dt_hi_made = sem("dt_hi_made")
        dt_made = sem("dt_made")
        z_done = sem("z_done")
        z_read = sem("z_read")
        gate_made = sem("gate_made")
        v_done = sem("v_done")
        v_capped = sem("v_capped")
        exp_done = sem("exp_done")
        log_done = sem("log_done")
        v_read = sem("v_read")
        y_made = sem("y_made")
        y_hi_made = sem("y_hi_made")
        y_parts_made = sem("y_parts_made")
        out_done = sem("out_done")
        x2_made = sem("x2_made")
        x2_out = [sem(f"x2_out{b}") for b in range(2)]
        var2_made = sem("var2_made")
        rstd2_made = sem("rstd2_made")
        xn2_made = sem("xn2_made")
        turned2 = sem("turned2")
        x2t_made = sem("x2t_made")
        logits_done = sem("logits_done")
        logits_read = sem("logits_read")
        chosen_made = sem("chosen_made")
        chosen_turned = sem("chosen_turned")
        chosen_read = sem("chosen_read")
        exps_made = sem("exps_made")
        table_made = sem("table_made")
        table_out = sem("table_out")
        block = ctx.enter_context(nc.Block())

        def each(eng, body):
            def one_pass(i):
                for b in range(2):
                    body(i * 2 + b, i, b)
            run_passes(eng, NG, one_pass)
            body(STEPS, NG, 0)

        def first(s):
            return known(s) and s == 0

        def early(s):
            return known(s) and s < 2

        def over(s):
            return known(s) and s >= STEPS

        def before(i, b):
            return (i, 0) if b == 1 else (i - 1, 1)

        @block.sync
        def _(sp):
            def body(s, i, b):
                if not first(s):
                    pi, pb = before(i, b)
                    if not over(s + 1):
                        sp.wait_ge(xn2_made, s)
                        sp.wait_ge(x2_out[pb], pi * 32 + 32)
                        sp.dma_start(X[pb][:, :, :], group(x1, pb, pi + 1)).then_inc(x_in[pb], 16)
            each(sp, body)
            for b in range(2):
                sp.wait_ge(x2_out[b], 32 * NG)
            sp.wait_ge(table_out, 16 * STEPS)

        def norm1(dve, s, i, b):
            dve.wait_ge(x_in[b], i * 16 + 16)
            row_stats(dve, X[b], stats, mv).then_inc(var_made, 1)
            dve.drain()
            dve.wait_ge(rstd_made, s + 1)
            normalise(dve, X[b], XN, mv, rstd).then_inc(xn_made, 1)

        def low_xt(dve, s, k):
            dve.wait_ge(xt_hi_made, s * KD + k + 1)
            dve.tensor_tensor(xt_lo[:, k, :], turn_ps[:, :], xt_hi[:, k, :], ALU.subtract)\
               .then_inc(xt_made, 1)

        @block.vector
        def _(dve):
            norm1(dve, 0, 0, 0)
            for k in range(KD):
                low_xt(dve, 0, k)

            def take_past(c, m, b):
                wait(dve, conv_made, c - 1)
                dve.tensor_copy(xs[m % 2][:, 0:PAST], past[b][:, m, :]).then_inc(past_in, 1)

            def convolve(c, m, b):
                t = temp[m % 2][:, :]
                dve.wait_ge(xs_read, c + 1)
                dve.wait_ge(past_in, c + 1)
                for tap in range(PAST):
                    conv = dve.scalar_tensor_tensor(
                        out=t, in0=xs[m % 2][:, tap:tap + GW], scalar=taps[:, m, tap:tap + 1],
                        in1=t, op0=ALU.mult, op1=ALU.add)
                    if tap < PAST - 1:
                        dve.drain()
                conv.then_inc(conv_made, 1)
                if m + 2 < MC:
                    take_past(c + 2, m + 2, b)

            def cap(v, m):
                dve.wait_ge(v_done, v + 1)
                if m >= 4:
                    dve.wait_ge(y_made, v - 3)
                dve.tensor_scalar(chain[m % 4][:, :], v_ps[m % 3][:, :], dt_bias[:, m:m + 1],
                                  SOFTPLUS_CAP, ALU.add, ALU.min).then_inc(v_capped, 1)

            def softplus(v, m):
                t = chain[m % 4][:, :]
                dve.wait_ge(log_done, v + 1)
                dve.scalar_tensor_tensor(out=t, in0=v_ps[m % 3][:, :], scalar=dt_bias[:, m:m + 1],
                                         in1=t, op0=ALU.add, op1=ALU.max).then_inc(v_read, 1)
                dve.wait_ge(v_read, v + 1)
                dve.wait_ge(gate_made, v + 1)
                dve.tensor_tensor(gated[:, m, :], gated[:, m, :], t, ALU.mult).then_inc(y_made, 1)

            def read_logits(s):
                dve.wait_ge(logits_done, s)
                dve.tensor_copy(router.flat(router.logits), turn_ps[:, 0:GT * E])\
                   .then_inc(logits_read, 1)

            def weigh(s):
                dve.wait_ge(exps_made, s + 1)
                router.weigh(dve, E).then_inc(table_made, 1)

            def keep_mask(s, i, b):
                dve.wait_ge(chosen_turned, s + 1)
                h = slice(64 * b, 64 * b + 64)
                dve.tensor_copy(windows[h, bass.ds(i * (GW // WIN), GW // WIN)],
                                turn_ps[h, 0:GW // WIN]).then_inc(chosen_read, 1)

            for m in range(2):
                take_past(m, m, 0)

            def body(s, i, b):
                pi, pb = before(i, b)
                if not first(s):
                    dve.wait_ge(out_done, s * MC)
                    for j in range(GT):
                        last = dve.tensor_tensor(X[pb][:, j, :], X[pb][:, j, :], out_ps[j][:, :], ALU.add)
                    last.then_inc(x2_made, 1)
                    dve.drain()
                    row_stats(dve, X[pb], stats, mv2).then_inc(var2_made, 1)
                if not over(s):
                    convolve(s * MC, 0, b)
                if not first(s):
                    if over(s):
                        dve.drain()
                    else:
                        wait(dve, turned, s * KD + KD)
                    dve.wait_ge(rstd2_made, s)
                    normalise(dve, X[pb], XN, mv2, rstd2).then_inc(xn2_made, 1)
                if not early(s):
                    keep_mask(s - 2, i - 1, b)
                if not over(s):
                    for m in range(1, MC):
                        convolve(s * MC + m, m, b)
                if not early(s):
                    weigh(s - 2)
                if not over(s):
                    dve.wait_ge(dt_hi_made, s + 1)
                    for c in (1, 3):
                        rows = slice(c * R, (c + 1) * R)
                        low = dve.tensor_tensor(dt_parts[rows, :], dt_ps[rows, :], dt_parts[rows, :],
                                                ALU.subtract)
                    low.then_inc(dt_made, 1)
                nb = 1 - b
                if not over(s + 1):
                    if first(s):
                        dve.wait_ge(turned, KD)
                        dve.wait_ge(res_made, 1)
                    else:
                        dve.wait_ge(turned2, s * KD)
                    norm1(dve, s + 1, i + b, nb)
                if not over(s):
                    v = s * MC
                    cap(v, 0)
                    cap(v + 1, 1)
                    dve.wait_ge(gate_made, v + MC)
                    cap(v + 2, 2)
                    for m in range(MC):
                        softplus(v + m, m)
                        if m == 0 and not first(s):
                            read_logits(s)
                        if 3 <= m + 2 < MC:
                            cap(v + m + 2, m + 2)
                        if not over(s + 1) and m - 1 in XT_TURNS:
                            low_xt(dve, s + 1, XT_TURNS.index(m - 1))
                if not first(s):
                    if over(s):
                        read_logits(s)
                    dve.drain()
                    router.pick(dve, E).then_inc(chosen_made, 1)
                    wait(dve, table_out, (s - 1) * 16)
                    router.keep_stats(dve, E, mv2, rstd2)
                if over(s):
                    weigh(s - 1)
                    keep_mask(s - 1, pi, pb)
                if not over(s + 1):
                    for m in range(2):
                        take_past((s + 1) * MC + m, m, nb)
            each(dve, body)

        @block.scalar
        def _(act):
            def high_xt(s, k):
                act.wait_ge(turned, s * KD + k + 1)
                act.activation(xt_hi[:, k, :], turn_ps[:, :], ACT.Copy).then_inc(xt_hi_made, 1)

            def copy_x2t(s, k):
                act.wait_ge(turned2, (s - 1) * KD + k + 1)
                act.activation(x2t[:, k, :], turn_ps[:, :], ACT.Copy).then_inc(x2t_made, 1)

            def silu_xc(c, m):
                act.wait_ge(conv_made, c + 1)
                act.activation(gated[:, m, :], temp[m % 2][:, :], ACT.Silu)
                if m < 2:
                    wait(act, out_done, c - 1)
                else:
                    act.wait_ge(xp_done, c - 1)
                act.activation(half_hi[m % 2][:, :], temp[m % 2][:, :], ACT.Silu)\
                   .then_inc(xc_hi_made, 1)

            def high_y(v, m):
                act.wait_ge(y_made, v + 1)
                if m >= 2:
                    act.wait_ge(out_done, v - 1)
                act.activation(half_hi[m % 2][:, :], gated[:, m, :], ACT.Copy).then_inc(y_hi_made, 1)

            for k in range(KD):
                high_xt(0, k)

            def body(s, i, b):
                for m in range(MC):
                    c = s * MC + m
                    if not first(s) and m >= 5:
                        copy_x2t(s, m - 5)
                    if not over(s):
                        act.wait_ge(xs_done, c + 1)
                        wait(act, conv_made, c - 1)
                        act.activation(xs[m % 2][:, PAST:PAST + GW], chunk_ps[m % 2][:, :], ACT.Copy)
                        act.wait_ge(past_in, c + 1)
                        act.activation(past[b][:, m, :], chunk_ps[m % 2][:, GW - PAST:GW], ACT.Copy)
                        if m < 2:
                            wait(act, y_made, c - 1)
                        else:
                            act.wait_ge(xc_hi_made, c - 1)
                        act.activation(temp[m % 2][:, :], chunk_ps[m % 2][:, :], ACT.Identity,
                                       bias=conv_bias[:, m:m + 1], scale=taps[:, m, PAST:PAST + 1])\
                           .then_inc(xs_read, 1)
                        if m >= 1:
                            silu_xc(c - 1, m - 1)
                if not first(s):
                    copy_x2t(s, KD - 1)
                if not over(s):
                    silu_xc(s * MC + MC - 1, MC - 1)
                    for m in range(MC):
                        c = s * MC + m
                        act.wait_ge(z_done, c + 1)
                        wait(act, gate_made, c - 1)
                        act.activation(silu_z[m % 2][:, :], chunk_ps[m % 2][:, :], ACT.Silu)\
                           .then_inc(z_read, 1)
                        if m == 4:
                            act.wait_ge(xp_done, (s + 1) * MC)
                            act.activation(dt_parts[:, :], dt_ps[:, :], ACT.Copy)\
                               .then_inc(dt_hi_made, 1)
                def exps():
                    act.wait_ge(chosen_made, s)
                    act.activation(router.flat(router.expd), router.flat(router.shifted), ACT.Exp)\
                       .then_inc(exps_made, 1)

                if over(s):
                    exps()
                    return
                act.preload_act_table_set("natural_log_exp_and_others")
                for m in range(MC):
                    v = s * MC + m
                    if m >= 2:
                        high_y(v - 2, m - 2)
                        if not over(s + 1) and m - 2 in XT_TURNS:
                            high_xt(s + 1, XT_TURNS.index(m - 2))
                    act.wait_ge(v_capped, v + 1)
                    act.activation(chain[m % 4][:, :], chain[m % 4][:, :], ACT.Exp).then_inc(exp_done, 1)
                    act.wait_ge(exp_done, v + 1)
                    act.activation(chain[m % 4][:, :], chain[m % 4][:, :], ACT.Ln, bias=1.0)\
                       .then_inc(log_done, 1)
                high_y(s * MC + MC - 2, MC - 2)
                high_y(s * MC + MC - 1, MC - 1)
                if not first(s):
                    exps()
            each(act, body)

        @block.gpsimd
        def _(pool):
            pool.wait_ge(var_made, 1)
            rstd_of(pool, mv, minus_half, rstd).then_inc(rstd_made, 1)
            pool.wait_ge(xn_made, 1)
            pool.tensor_tensor(X[0][:, :, :], X[0][:, :, :], XN[:, :, :], ALU.add).then_inc(res_made, 1)

            def store_table(s, i, b):
                pool.wait_ge(table_made, s + 1)
                pool.dma_start(group(tab2, b, i), router.table[:, :, :]).then_inc(table_out, 16)

            def body(s, i, b):
                pi, pb = before(i, b)

                def low_xc(m):
                    pool.wait_ge(xc_hi_made, s * MC + m + 1)
                    pool.tensor_tensor(half_lo[m % 2][:, :], gated[:, m, :], half_hi[m % 2][:, :],
                                       ALU.subtract).then_inc(xc_made, 1)

                def store_x2(rows):
                    pool.dma_start(group(rows, pb, pi), X[pb][:, :, :]).then_inc(x2_out[pb], 16)

                if not first(s):
                    pool.wait_ge(var2_made, s)
                    rstd_of(pool, mv2, minus_half, rstd2).then_inc(rstd2_made, 1)
                if over(s):
                    store_x2(x2)
                    store_x2(out_rows)
                    store_table(s - 2, i - 1, b)
                    store_table(s - 1, pi, pb)
                    return
                for m in range(MC):
                    low_xc(m)
                    if not first(s) and m in (2, 3):
                        store_x2((x2, out_rows)[m - 2])
                for m in range(MC):
                    c = s * MC + m
                    pool.wait_ge(z_read, c + 1)
                    pool.wait_ge(xc_made, c + 1)
                    pool.tensor_tensor(gated[:, m, :], gated[:, m, :], silu_z[m % 2][:, :], ALU.mult)\
                        .then_inc(gate_made, 1)
                    if m == 4 and not over(s + 1):
                        pool.wait_ge(var_made, s + 2)
                        rstd_of(pool, mv, minus_half, rstd).then_inc(rstd_made, 1)
                if not early(s):
                    store_table(s - 2, i - 1, b)
                for m in range(MC):
                    v = s * MC + m
                    pool.wait_ge(y_hi_made, v + 1)
                    pool.tensor_tensor(half_lo[m % 2][:, :], gated[:, m, :], half_hi[m % 2][:, :],
                                       ALU.subtract).then_inc(y_parts_made, 1)
                    if not over(s + 1) and m < GT:
                        if m == 0:
                            pool.wait_ge(xn_made, s + 2)
                        n = 1 - b
                        part = pool.tensor_tensor(X[n][:, m, :], X[n][:, m, :], XN[:, m, :], ALU.add)
                        if m == GT - 1:
                            part.then_inc(res_made, 1)
            each(pool, body)

        @block.tensor
        def _(pe):
            def three(bank, a, b, start, stop):
                pe.matmul(bank, a[0], b[0], start=start, stop=False)
                pe.matmul(bank, a[0], b[1], start=False, stop=False)
                return pe.matmul(bank, a[1], b[0], start=False, stop=stop)

            def turn(src, k):
                for j in range(GT):
                    mm = pe.transpose(turn_ps[:, j * P:(j + 1) * P], src[:, j, k * P:(k + 1) * P],
                                      ident[:, :])
                return mm

            def turn_xt(s, k):
                if k == 0:
                    pe.wait_ge(xn_made, s + 1)
                    wait(pe, logits_read, s - 1)
                else:
                    pe.wait_ge(xt_made, s * KD + k)
                turn(XN, k).then_inc(turned, 1)

            def in_proj(m):
                for k in range(KD):
                    cols = slice(m * P, (m + 1) * P)
                    mm = three(chunk_ps[m % 2][:, :], (w_in_hi[:, k, cols], w_in_lo[:, k, cols]),
                               (xt_hi[:, k, :], xt_lo[:, k, :]), k == 0, k == KD - 1)
                return mm

            def x_proj(s, m):
                wx, hi, lo = (w_x_hi[:, m, :], w_x_lo[:, m, :]), half_hi[m % 2], half_lo[m % 2]
                pe.wait_ge(xc_hi_made, s * MC + m + 1)
                pe.matmul(dt_ps[:, :], wx[0], hi[:, :], start=m == 0, stop=False)
                pe.matmul(dt_ps[:, :], wx[1], hi[:, :], start=False, stop=False)
                pe.wait_ge(xc_made, s * MC + m + 1)
                pe.matmul(dt_ps[:, :], wx[0], lo[:, :], start=False, stop=m == MC - 1)\
                    .then_inc(xp_done, 1)

            def out_proj(s, m):
                pe.wait_ge(y_hi_made, s * MC + m + 1)
                if m == 0:
                    wait(pe, x2_made, s)
                for j in range(GT):
                    hi = half_hi[m % 2][:, j * P:(j + 1) * P]
                    pe.matmul(out_ps[j][:, :], hi, w_out_hi[:, m, :], start=m == 0, stop=False)
                    pe.matmul(out_ps[j][:, :], hi, w_out_lo[:, m, :], start=False, stop=False)
                pe.wait_ge(y_parts_made, s * MC + m + 1)
                for j in range(GT):
                    mm = pe.matmul(out_ps[j][:, :], half_lo[m % 2][:, j * P:(j + 1) * P],
                                   w_out_hi[:, m, :], start=False, stop=m == MC - 1)
                mm.then_inc(out_done, 1)

            def dt_proj(s, m):
                v = s * MC + m
                if m == 0:
                    pe.wait_ge(dt_made, s + 1)
                elif m < 3:
                    pe.wait_ge(z_read, s * MC + MC - 2 + m)
                else:
                    pe.wait_ge(v_read, v - 2)
                pe.matmul(v_ps[m % 3][:, :], w_dt_parts[:, m * P:(m + 1) * P], dt_parts[:, :],
                          start=True, stop=True).then_inc(v_done, 1)

            for k in range(KD):
                turn_xt(0, k)

            def body(s, i, b):
                pb = before(i, b)[1]
                for m in range(MC):
                    if not over(s):
                        c = s * MC + m
                        if m == 0:
                            pe.wait_ge(xt_made, (s + 1) * KD)
                            wait(pe, v_read, s * MC)
                        elif m >= 2:
                            pe.wait_ge(xs_read, c - 1)
                        in_proj(m).then_inc(xs_done, 1)
                        if m >= 3:
                            x_proj(s, m - 3)
                    if not early(s) and m == 2:
                        pe.wait_ge(chosen_made, s - 1)
                        if over(s):
                            pe.wait_ge(xt_made, s * KD)
                        turn_mask(pe, turn_ps, router, win_bits, b).then_inc(chosen_turned, 1)
                    if not first(s) and m >= MC - KD:
                        k = m - (MC - KD)
                        if k == 0:
                            pe.wait_ge(xn2_made, s)
                            if not early(s):
                                pe.wait_ge(chosen_read, s - 1)
                        else:
                            pe.wait_ge(x2t_made, (s - 1) * KD + k)
                        turn(XN, k).then_inc(turned2, 1)
                for m in range(MC):
                    if not over(s):
                        c = s * MC + m
                        if m < 2:
                            pe.wait_ge(xs_read, c + MC - 1)
                        else:
                            pe.wait_ge(z_read, c - 1)
                        in_proj(MC + m).then_inc(z_done, 1)
                        if m < 3:
                            x_proj(s, MC - 3 + m)
                        if m == MC - 2:
                            dt_proj(s, 0)
                if not over(s):
                    dt_proj(s, 1)
                    dt_proj(s, 2)
                if not first(s):
                    pe.wait_ge(x2t_made, s * KD)
                    logits(pe, turn_ps, x2t, gate_sb, KD, E).then_inc(logits_done, 1)
                if over(s):
                    pe.wait_ge(chosen_made, s)
                    turn_mask(pe, turn_ps, router, win_bits, pb).then_inc(chosen_turned, 1)
                    return
                for m in range(MC):
                    if not over(s + 1) and m in XT_TURNS:
                        turn_xt(s + 1, XT_TURNS.index(m))
                    if m + 3 < MC:
                        dt_proj(s, m + 3)
                    out_proj(s, m)
            each(pe, body)


def kernel(**inputs):
    import numpy as np
    import concourse.bacc as bacc
    from concourse import mybir as m
    from concourse.bass_utils import run_bass_kernel_spmd

    a = {name.removeprefix("L0_"): np.asarray(value) for name, value in inputs.items()}

    def rows_on_partitions(w):
        return np.ascontiguousarray(w.reshape(-1, P, w.shape[1]).transpose(1, 0, 2))

    E, inner, D = a["ffn_w_gate"].shape
    R = a["attn_W_dt"].shape[1]
    gate_up = np.stack([a["ffn_w_gate"], a["ffn_w_up"]], 1)
    gate_up = gate_up.reshape(E, 2, inner, D // P, P).transpose(0, 4, 1, 3, 2).reshape(E, P, -1)
    down = a["ffn_w_down"].reshape(E, D, inner // P, P).transpose(0, 3, 2, 1).reshape(E, P, -1)
    arrays = {
        "x": a["attn_x"],
        "moe_w": np.ascontiguousarray(np.concatenate([gate_up, down], 2)),
        "gate_t": rows_on_partitions(a["ffn_gate_w"].T),
        "w_in": rows_on_partitions(a["attn_W_in"].T),
        "w_out": rows_on_partitions(a["attn_W_out"].T),
        "w_x": rows_on_partitions(a["attn_W_x"][:R].T),
        "w_dt": np.ascontiguousarray(a["attn_W_dt"].T),
        "conv_w": rows_on_partitions(a["attn_conv_w"][:, 0, :]),
        "conv_b": np.ascontiguousarray(a["attn_conv_b"].reshape(-1, P).T),
        "b_dt": np.ascontiguousarray(a["attn_b_dt"].reshape(-1, P).T),
    }
    nc = bacc.Bacc("TRN2", target_bir_lowering=False, num_devices=1)
    aps = {name: nc.dram_tensor(name, v.shape, m.dt.from_np(v.dtype), kind="ExternalInput").ap()
           for name, v in arrays.items()}
    shape = arrays["x"].shape
    out = nc.dram_tensor("out", shape, m.dt.float32, kind="ExternalOutput").ap()
    build_program(nc, out=out, **aps)
    result = run_bass_kernel_spmd(nc, [arrays], core_ids=[0])
    return result.results[0]["out"]
```
